# Optimizing a Trainium2 kernel written in Bass

```python
import numpy as np
import jax
import jax.numpy as jnp

def _softmax(x, axis=-1):
    return jax.nn.softmax(x, axis=axis)

def _gelu(x):
    return jax.nn.gelu(x, approximate=True)

def _silu(x):
    return jax.nn.silu(x)

def _sigmoid(x):
    return jax.nn.sigmoid(x)

def _layernorm(x, axis=-1, eps=1e-05):
    m = jnp.mean(x, axis=axis, keepdims=True)
    v = jnp.var(x, axis=axis, keepdims=True)
    return (x - m) / jnp.sqrt(v + eps)

def _scatter_add(tgt, idx, src, axis=0):
    return tgt.at[idx].add(src)

def _segment_sum(src, seg, n):
    return jax.ops.segment_sum(src, seg, n)
kernel_name = 'mk_macaron_d1_jaxref_r8_5e2197'

def setup_inputs(seed: int=0):
    np.random.seed(seed)
    _w = jnp.asarray

    def _L0_attn_setup():
        import jax, jax.numpy as jnp
        import numpy as np
        B, S, D = (2, 512, 256)
        H, HKV, DH = (16, 4, 128)
        CHUNK = 64
        GROUPS = H // HKV

        def _alibi_slopes(n_heads):
            i = jnp.arange(1, n_heads + 1, dtype=jnp.float32)
            return jnp.exp2(-8.0 * i / n_heads)

        def _rope(x):
            s, d = (x.shape[2], x.shape[3])
            inv_freq = 1.0 / 10000.0 ** (jnp.arange(0, d, 2, dtype=jnp.float32) / d)
            freqs = jnp.arange(s, dtype=jnp.float32)[:, None] * inv_freq[None, :]
            cos = jnp.concatenate([jnp.cos(freqs), jnp.cos(freqs)], axis=-1)
            sin = jnp.concatenate([jnp.sin(freqs), jnp.sin(freqs)], axis=-1)
            x1, x2 = (x[..., :d // 2], x[..., d // 2:])
            rot = jnp.concatenate([-x2, x1], axis=-1)
            return x * cos[None, None] + rot * sin[None, None]

        def _lightning_attn(q, k, v):
            b, h, s, dh = q.shape
            nc = s // CHUNK
            lam = _alibi_slopes(h)
            r = jnp.arange(CHUNK, dtype=jnp.float32)
            diff = r[:, None] - r[None, :]
            diag = jnp.where(diff >= 0, jnp.exp(-lam[:, None, None] * diff), 0.0)
            q_dec = jnp.exp(-lam[:, None] * (r + 1.0))
            k_dec = jnp.exp(-lam[:, None] * (CHUNK - 1.0 - r))
            blk = jnp.exp(-lam * CHUNK)
            qc = q.reshape(b, h, nc, CHUNK, dh).transpose(2, 0, 1, 3, 4)
            kc = k.reshape(b, h, nc, CHUNK, dh).transpose(2, 0, 1, 3, 4)
            vc = v.reshape(b, h, nc, CHUNK, dh).transpose(2, 0, 1, 3, 4)

            def step(kv, inp):
                qi, ki, vi = inp
                scores = jnp.einsum('bhid,bhjd->bhij', qi, ki) * diag[None]
                o_intra = jnp.einsum('bhij,bhje->bhie', scores, vi)
                o_inter = jnp.einsum('bhid,bhde->bhie', qi * q_dec[None, :, :, None], kv)
                kv = blk[None, :, None, None] * kv + jnp.einsum('bhjd,bhje->bhde', ki * k_dec[None, :, :, None], vi)
                return (kv, o_intra + o_inter)
            kv0 = jnp.zeros((b, h, dh, dh), q.dtype)
            _, o = jax.lax.scan(step, kv0, (qc, kc, vc))
            return o.transpose(1, 2, 0, 3, 4).reshape(b, h, s, dh)
        key = jax.random.key(seed)
        ks = jax.random.split(key, 5)
        sc = 0.02
        return {'x': jax.random.normal(ks[0], (B, S, D), jnp.float32), 'wq': jax.random.normal(ks[1], (H * DH, D), jnp.float32) * sc, 'wk': jax.random.normal(ks[2], (HKV * DH, D), jnp.float32) * sc, 'wv': jax.random.normal(ks[3], (HKV * DH, D), jnp.float32) * sc, 'wo': jax.random.normal(ks[4], (D, H * DH), jnp.float32) * sc}
    _L0_attn_in = _L0_attn_setup()

    def _L0_ffn_setup():
        import jax, jax.numpy as jnp
        import numpy as np
        HIDDEN = 256
        NUM_EXPERTS = 32
        TOP_K = 4
        MOE_INTER = 96
        GROUP = 2
        NUM_CHUNK = NUM_EXPERTS // GROUP
        CHUNK_INTER = 128
        SMALL_SCALE = 0.05

        def _routing(x2d, gate_w):
            logits = x2d @ gate_w.T
            rw = jax.nn.softmax(logits.astype(jnp.float32), axis=-1)
            scores = jax.nn.sigmoid(logits.astype(jnp.float32))
            _, sel = jax.lax.top_k(scores, TOP_K)
            w = jnp.take_along_axis(rw, sel, axis=-1)
            w = w / w.sum(axis=-1, keepdims=True)
            return (w.astype(x2d.dtype), sel)

        def _moe(x2d, Wg, Wu, Wd, cw):
            g = jnp.einsum('th,ehi->eti', x2d, Wg)
            u = jnp.einsum('th,ehi->eti', x2d, Wu)
            a = jax.nn.silu(g) * u * cw.T[:, :, None]
            return jnp.einsum('eti,eih->th', a, Wd)
        key = jax.random.key(seed)
        ks = jax.random.split(key, 8)
        s = 0.02
        B, S = (2, 256)
        return {'hidden_states': jax.random.normal(ks[0], (B, S, HIDDEN), jnp.float32), 'gate_w': jax.random.normal(ks[1], (NUM_EXPERTS, HIDDEN), jnp.float32) * s, 'Wg': jax.random.normal(ks[2], (NUM_EXPERTS, HIDDEN, MOE_INTER), jnp.float32) * s, 'Wu': jax.random.normal(ks[3], (NUM_EXPERTS, HIDDEN, MOE_INTER), jnp.float32) * s, 'Wd': jax.random.normal(ks[4], (NUM_EXPERTS, MOE_INTER, HIDDEN), jnp.float32) * s, 'cWg': jax.random.normal(ks[5], (NUM_CHUNK, HIDDEN, CHUNK_INTER), jnp.float32) * s, 'cWu': jax.random.normal(ks[6], (NUM_CHUNK, HIDDEN, CHUNK_INTER), jnp.float32) * s, 'cWd': jax.random.normal(ks[7], (NUM_CHUNK, CHUNK_INTER, HIDDEN), jnp.float32) * s}
    _L0_ffn_in = _L0_ffn_setup()
    _d = {'L0_attn_x': _L0_attn_in['x'], 'L0_attn_wq': _L0_attn_in['wq'], 'L0_attn_wk': _L0_attn_in['wk'], 'L0_attn_wv': _L0_attn_in['wv'], 'L0_attn_wo': _L0_attn_in['wo'], 'L0_ffn_gate_w': _L0_ffn_in['gate_w'], 'L0_ffn_Wg': _L0_ffn_in['Wg'], 'L0_ffn_Wu': _L0_ffn_in['Wu'], 'L0_ffn_Wd': _L0_ffn_in['Wd'], 'L0_ffn_cWg': _L0_ffn_in['cWg'], 'L0_ffn_cWu': _L0_ffn_in['cWu'], 'L0_ffn_cWd': _L0_ffn_in['cWd']}
    _x0 = _d['L0_attn_x']
    _d['L0_attn_x'] = jax.random.normal(jax.random.fold_in(jax.random.key(seed), 1), (2, 512, 256), dtype=_x0.dtype)
    del _x0
    return _d

def reference(L0_attn_x, L0_attn_wq, L0_attn_wk, L0_attn_wv, L0_attn_wo, L0_ffn_gate_w, L0_ffn_Wg, L0_ffn_Wu, L0_ffn_Wd, L0_ffn_cWg, L0_ffn_cWu, L0_ffn_cWd):

    def _L0_attn_ref(x, wq, wk, wv, wo):
        import jax, jax.numpy as jnp
        import numpy as np
        B, S, D = (2, 512, 256)
        H, HKV, DH = (16, 4, 128)
        CHUNK = 64
        GROUPS = H // HKV

        def _alibi_slopes(n_heads):
            i = jnp.arange(1, n_heads + 1, dtype=jnp.float32)
            return jnp.exp2(-8.0 * i / n_heads)

        def _rope(x):
            s, d = (x.shape[2], x.shape[3])
            inv_freq = 1.0 / 10000.0 ** (jnp.arange(0, d, 2, dtype=jnp.float32) / d)
            freqs = jnp.arange(s, dtype=jnp.float32)[:, None] * inv_freq[None, :]
            cos = jnp.concatenate([jnp.cos(freqs), jnp.cos(freqs)], axis=-1)
            sin = jnp.concatenate([jnp.sin(freqs), jnp.sin(freqs)], axis=-1)
            x1, x2 = (x[..., :d // 2], x[..., d // 2:])
            rot = jnp.concatenate([-x2, x1], axis=-1)
            return x * cos[None, None] + rot * sin[None, None]

        def _lightning_attn(q, k, v):
            b, h, s, dh = q.shape
            nc = s // CHUNK
            lam = _alibi_slopes(h)
            r = jnp.arange(CHUNK, dtype=jnp.float32)
            diff = r[:, None] - r[None, :]
            diag = jnp.where(diff >= 0, jnp.exp(-lam[:, None, None] * diff), 0.0)
            q_dec = jnp.exp(-lam[:, None] * (r + 1.0))
            k_dec = jnp.exp(-lam[:, None] * (CHUNK - 1.0 - r))
            blk = jnp.exp(-lam * CHUNK)
            qc = q.reshape(b, h, nc, CHUNK, dh).transpose(2, 0, 1, 3, 4)
            kc = k.reshape(b, h, nc, CHUNK, dh).transpose(2, 0, 1, 3, 4)
            vc = v.reshape(b, h, nc, CHUNK, dh).transpose(2, 0, 1, 3, 4)

            def step(kv, inp):
                qi, ki, vi = inp
                scores = jnp.einsum('bhid,bhjd->bhij', qi, ki) * diag[None]
                o_intra = jnp.einsum('bhij,bhje->bhie', scores, vi)
                o_inter = jnp.einsum('bhid,bhde->bhie', qi * q_dec[None, :, :, None], kv)
                kv = blk[None, :, None, None] * kv + jnp.einsum('bhjd,bhje->bhde', ki * k_dec[None, :, :, None], vi)
                return (kv, o_intra + o_inter)
            kv0 = jnp.zeros((b, h, dh, dh), q.dtype)
            _, o = jax.lax.scan(step, kv0, (qc, kc, vc))
            return o.transpose(1, 2, 0, 3, 4).reshape(b, h, s, dh)
        b, s, _ = x.shape
        q = jnp.einsum('bsd,ed->bse', x, wq).reshape(b, s, H, DH).transpose(0, 2, 1, 3)
        k = jnp.einsum('bsd,ed->bse', x, wk).reshape(b, s, HKV, DH).transpose(0, 2, 1, 3)
        v = jnp.einsum('bsd,ed->bse', x, wv).reshape(b, s, HKV, DH).transpose(0, 2, 1, 3)
        q = _rope(q)
        k = _rope(k)
        k = jnp.repeat(k, GROUPS, axis=1)
        v = jnp.repeat(v, GROUPS, axis=1)
        o = _lightning_attn(q, k, v)
        o = o.transpose(0, 2, 1, 3).reshape(b, s, H * DH)
        return jnp.einsum('bse,de->bsd', o, wo)

    def _L0_ffn_ref(hidden_states, gate_w, Wg, Wu, Wd, cWg, cWu, cWd):
        import jax, jax.numpy as jnp
        import numpy as np
        HIDDEN = 256
        NUM_EXPERTS = 32
        TOP_K = 4
        MOE_INTER = 96
        GROUP = 2
        NUM_CHUNK = NUM_EXPERTS // GROUP
        CHUNK_INTER = 128
        SMALL_SCALE = 0.05

        def _routing(x2d, gate_w):
            logits = x2d @ gate_w.T
            rw = jax.nn.softmax(logits.astype(jnp.float32), axis=-1)
            scores = jax.nn.sigmoid(logits.astype(jnp.float32))
            _, sel = jax.lax.top_k(scores, TOP_K)
            w = jnp.take_along_axis(rw, sel, axis=-1)
            w = w / w.sum(axis=-1, keepdims=True)
            return (w.astype(x2d.dtype), sel)

        def _moe(x2d, Wg, Wu, Wd, cw):
            g = jnp.einsum('th,ehi->eti', x2d, Wg)
            u = jnp.einsum('th,ehi->eti', x2d, Wu)
            a = jax.nn.silu(g) * u * cw.T[:, :, None]
            return jnp.einsum('eti,eih->th', a, Wd)
        B, S, H = hidden_states.shape
        T = B * S
        x = hidden_states.reshape(T, H)
        w, sel = _routing(x, gate_w)
        rows = jnp.arange(T)[:, None]
        cw_large = jnp.zeros((T, NUM_EXPERTS), x.dtype).at[rows, sel].add(w)
        cw_small = jnp.zeros((T, NUM_CHUNK), x.dtype).at[rows, sel // GROUP].add(w)
        large = _moe(x, Wg, Wu, Wd, cw_large)
        small = _moe(x, cWg, cWu, cWd, cw_small)
        return (large + SMALL_SCALE * small).reshape(B, S, H)
    x = L0_attn_x
    x = x + 0.5 * _L0_ffn_ref(_layernorm(x, axis=-1), L0_ffn_gate_w, L0_ffn_Wg, L0_ffn_Wu, L0_ffn_Wd, L0_ffn_cWg, L0_ffn_cWu, L0_ffn_cWd)
    x = x + _L0_attn_ref(_layernorm(x, axis=-1), L0_attn_wq, L0_attn_wk, L0_attn_wv, L0_attn_wo)
    x = x + 0.5 * _L0_ffn_ref(_layernorm(x, axis=-1), L0_ffn_gate_w, L0_ffn_Wg, L0_ffn_Wu, L0_ffn_Wd, L0_ffn_cWg, L0_ffn_cWu, L0_ffn_cWd)
    return x

_drawn_inputs = setup_inputs


def setup_inputs(seed=0):
    import zlib

    import numpy as np

    out = dict(_drawn_inputs(seed))
    spreads = {}
    factors = {'L0_ffn_gate_w': 8.0,
     'L0_ffn_Wg': 8.0,
     'L0_ffn_Wu': 8.0,
     'L0_ffn_Wd': 8.0,
     'L0_ffn_cWg': 8.0,
     'L0_ffn_cWu': 8.0,
     'L0_ffn_cWd': 8.0}
    for name, (base, spread) in spreads.items():
        noise = np.random.default_rng([zlib.crc32(name.encode()), seed]).standard_normal(out[name].shape)
        drawn = base * np.exp(spread * noise) if base else spread * noise
        out[name] = jnp.asarray(drawn.astype(out[name].dtype))
    for name, factor in factors.items():
        out[name] = (out[name] * factor).astype(out[name].dtype)
    return out
```

```python
import numpy as np
import concourse.bass as bass
from concourse import mybir
from contextlib import ExitStack

P = 128
B, S, D = 2, 512, 256
T = B * S
TT = T // P
SB = S // P
KD = D // P
H, HKV, DH = 16, 4, 128
GROUPS = H // HKV
E, TOP_K, MI = 32, 4, 96
NCH, CI = 16, 128
SMALL_SCALE = 0.05
EPS = 1e-5
SLOT_TILES = T * TOP_K // P + E
XG, YG = 4, 8
WI = MI + CI
EXP_COLS = 2 * 2 * MI
CH_COLS = 2 * CI
CHUNK_BYTES_COLS = KD * EXP_COLS + KD * CH_COLS + D
LN_EPS = EPS


def macaron_kernel(nc, x_in, gate, w_up, w_down, wq, wk, wv, wo, decay, cos, sin, ident, tri, iotas, scan_keep, out):
    f32, f16, i32, u32 = mybir.dt.float32, mybir.dt.float16, mybir.dt.int32, mybir.dt.uint32
    ALU = mybir.AluOpType
    ACT = mybir.ActivationFunctionType
    AX = mybir.AxisListType

    ctx = ExitStack()
    with ctx:
        def sb(name, shape, dt=f32):
            return ctx.enter_context(nc.sbuf_tensor(name, shape, dt))

        def sem(name):
            return ctx.enter_context(nc.semaphore(name))

        def sems(name, n):
            return [sem(f"{name}{i}") for i in range(n)]

        xn_dram = [nc.dram_tensor(f"xn_dram{l}", (T, D), f32).ap() for l in range(2)]
        y_dram = [nc.dram_tensor(f"y_dram{l}", (SLOT_TILES * P, D), f32).ap() for l in range(2)]

        w_up_sb = sb("w_up_sb", [P, NCH * CHUNK_BYTES_COLS])
        w_down_sb = sb("w_down_sb", [MI, E * D])
        gate_sb = sb("gate_sb", [P, KD, E])
        x_sb = sb("x_sb", [P, TT, D])
        xn_sb = sb("xn_sb", [P, TT, D])
        xnT = sb("xnT", [P, KD, T])
        ident_sb = sb("ident_sb", [P, P])
        tri_sb = sb("tri_sb", [P, 2, P], f16)
        iota_sb = sb("iota_sb", [P, P])
        tok_sb = sb("tok_sb", [P, TT * TOP_K])
        thr_sb = sb("thr_sb", [P, TT])
        scan_keep_sb = sb("scan_keep_sb", [P, E * TT])
        stats = sb("stats", [P, 6])
        mv = sb("mv", [P, TT, 2])
        var_eps = sb("var_eps", [P, TT])
        rvar = sb("rvar", [P, TT])
        rstd = sb("rstd", [P, TT])

        lg = sb("lg", [P, TT, E])
        top = sb("top", [P, TT, 8])
        top_ix = sb("top_ix", [P, TT, 8], u32)
        ixf = sb("ixf", [P, TT, TOP_K])
        member = sb("member", [P, TT, E], f16)
        top_rel = sb("top_rel", [P, TT, TOP_K])
        top_exp = sb("top_exp", [P, TT, TOP_K])
        top_sum = sb("top_sum", [P, TT])
        wgt = sb("wgt", [P, TT, TOP_K])
        ntile = sb("ntile", [P, E])
        ntile_incl = sb("ntile_incl", [P, E])
        ntile_excl = sb("ntile_excl", [P, E])
        ones_e = sb("ones_e", [P, E])
        slot_base = sb("slot_base", [P, E, TT])
        slot_te = sb("slot_te", [P, TT, E])
        slotf = sb("slotf", [P, TT * TOP_K])
        slot_ix = sb("slot_ix", [P, TT * TOP_K], i32)
        slot_qi = sb("slot_qi", [P, TT * TOP_K], i32)
        slot_ri = sb("slot_ri", [P, TT * TOP_K], i32)
        slot_q = sb("slot_q", [P, TT * TOP_K])
        slot_r = sb("slot_r", [P, TT * TOP_K])
        tile_e = sb("tile_e", [1, SLOT_TILES])
        tile_e_i = sb("tile_e_i", [1, SLOT_TILES], i32)
        tile_c_i = sb("tile_c_i", [1, SLOT_TILES], i32)
        ids = sb("ids", [P, SLOT_TILES], i32)

        ids_col = [sb(f"ids_col{u}", [P, 1], i32) for u in range(XG)]
        y_sb = [sb(f"y_sb{u}", [P, D]) for u in range(2)]

        rot = sb("rot", [P, 2, S])
        cos_sb, sin_sb = rot[:, 0, :], rot[:, 1, :]
        wkv_sb = sb("wkv_sb", [P, 2, KD, DH])
        wk_sb, wv_sb = wkv_sb[:, 0, :, :], wkv_sb[:, 1, :, :]
        wq_all = sb("wq_all", [P, 2, KD, DH])
        wq_sb = [wq_all[:, u, :, :] for u in range(2)]
        wo_all = sb("wo_all", [P, 2, D])
        wo_sb = [wo_all[:, u, :] for u in range(2)]
        decay_all = sb("decay_all", [P, 2, S])
        decay_sb = [decay_all[:, u, :] for u in range(2)]
        rope = sb("rope", [P, 4, S])
        rope_a, rope_b = [rope[:, u, :] for u in range(2)], [rope[:, 2 + u, :] for u in range(2)]
        kqT = sb("kqT", [P, 4, S])
        kT, qT = [kqT[:, b, :] for b in range(B)], [kqT[:, 2 + u, :] for u in range(2)]
        v_all = sb("v_all", [P, TT * DH])
        v_sb = v_all[:, :].rearrange("p (t d) -> p t d", t=TT)
        probs_all = sb("probs_all", [P, SB * (SB + 1) // 2 * P])
        probs = [probs_all[:, j * S - j * (j - 1) // 2 * P:(j + 1) * S - (j + 1) * j // 2 * P] for j in range(SB)]
        oT_all = sb("oT_all", [P, 2 * S])
        oT = [oT_all[:, u * S:(u + 1) * S] for u in range(2)]
        chosen = probs_all[:, 0:TT * TOP_K * E].rearrange("p (t k e) -> p t k e", t=TT, k=TOP_K)
        tot, over = [wo_all[:, a, :].rearrange("p (e t) -> p e t", t=TT) for a in range(2)]
        tot_incl, tot_excl = [wq_all[:, a, :, :].rearrange("p k n -> p (k n)").rearrange("p (e t) -> p e t", t=TT)
                              for a in range(2)]
        xg = [decay_all[:, u // 2, (u % 2) * D:(u % 2 + 1) * D] for u in range(XG)]
        xgT = [oT_all[:, u * D:(u + 1) * D].rearrange("p (k t) -> p k t", k=KD) for u in range(2)]
        silu_g = [rot[:, 0, u * WI:(u + 1) * WI] for u in range(2)]
        act = [rot[:, 1, u * WI:(u + 1) * WI] for u in range(2)]
        actT = [wkv_sb[:, u, :, :] for u in range(2)]
        yg = [kqT[:, u // 2, (u % 2) * D:(u % 2 + 1) * D] for u in range(YG)]
        hot_r = rope[:, :, :].rearrange("p a s -> p (a s)").bitcast(f16).rearrange("p (n r) -> p n r", r=P)
        hot_q = v_all[:, :].bitcast(f16).rearrange("p (n q) -> p n q", q=SLOT_TILES)
        slot_pick = oT_all[:, :].rearrange("p (t k e) -> p t k e", t=TT, k=TOP_K)
        tile_ge = kqT[0:1, :, :].rearrange("p a s -> p (a s)").rearrange("p (t e) -> p t e", e=E)

        bank = [ctx.enter_context(nc.psum_tensor(f"bank{i}", [P, 512], f32)) for i in range(8)]
        xT_ps = [bank[0], bank[1]]
        logit_ps, rank_ps, tot_ps, ids_ps = bank[2], bank[3], bank[4], bank[5]
        h_ps, aT_ps, y_ps = [bank[2], bank[3]], [bank[4], bank[5]], [bank[6], bank[7]]
        proj_ps, o_ps, sc_ps = bank[0], bank[1], [bank[2], bank[3]]
        res_ps = [bank[4 + i // 2][:, (i % 2) * D:(i % 2 + 1) * D] for i in range(TT)]

        const_in = sem("const_in")
        x_loaded = sems("x_loaded", TT)
        w_in = sems("w_in", NCH)
        w_ready = sem("w_ready")
        dve_step = sem("dve_step")
        rvar_ready, rstd_ready = sem("rvar_ready"), sem("rstd_ready")
        xn_ready, xnT_mm, xnT_copied = sem("xn_ready"), sem("xnT_mm"), sem("xnT_copied")
        xn_stored = sems("xn_stored", 2)
        logits_mm, lg_ready = sem("logits_mm"), sem("lg_ready")
        rel_ready, exp_ready = sem("rel_ready"), sem("exp_ready")
        member_ready, rank_mm = sem("member_ready"), sem("rank_mm")
        slots_ready, hot_q_ready, hot_r_ready = sem("slots_ready"), sem("hot_q_ready"), sem("hot_r_ready")
        ids_mm, ids_ready, tiles_ready = sem("ids_mm"), sem("ids_ready"), sem("tiles_ready")
        col_ready, waits_passed = sem("col_ready"), sem("waits_passed")
        xg_ready, xg_used = sems("xg_ready", XG), sems("xg_used", XG)
        xgT_ready = sems("xgT_ready", 2)
        h_mm, silu_ready, act_ready = sems("h_mm", 2), sems("silu_ready", 2), sems("act_ready", 2)
        actT_mm, actT_ready = sems("actT_mm", 2), sems("actT_ready", 2)
        y_mm, y_ready, y_stored = sems("y_mm", 2), sems("y_ready", 2), sems("y_stored", 2)
        yg_ready, yg_used = sems("yg_ready", YG), sems("yg_used", YG)
        x_done = sem("x_done")
        out_stored = sem("out_stored")
        kv_in, wq_in, wo_in, decay_in = sem("kv_in"), sems("wq_in", 2), sems("wo_in", 2), sems("decay_in", 2)
        v_mm, v_copied = sem("v_mm"), sem("v_copied")
        proj_mm, rope_read, roped = sem("proj_mm"), sem("rope_read"), sems("roped", 2)
        scores_mm, scores_done, masked = sem("scores_mm"), sem("scores_done"), sems("masked", 2)
        pv_mm, o_copied, wo_mm = sem("pv_mm"), sem("o_copied"), sems("wo_mm", 2)
        x2_copied = sem("x2_copied")

        N_CONST = 8

        UNROLL = XG
        ROUNDS = SLOT_TILES // UNROLL

        def slot_of(l, it, u, d, buffers=2):
            v = u + d
            return v % buffers, (it + l * ROUNDS) * (UNROLL // buffers) + (v // buffers + 1)

        def expert_steps(eng, step, first, last):
            lo, hi = 1, ROUNDS - 1
            for t in range(first, UNROLL * lo):
                step(t // UNROLL, t % UNROLL, t)
            with eng.Fori(lo, hi) as it:
                for u in range(UNROLL):
                    step(it, u, None)
            for t in range(UNROLL * hi, last):
                step(t // UNROLL, t % UNROLL, t)

        block = ctx.enter_context(nc.Block())

        def store_results(sp, l):
            with sp.Fori(0, ROUNDS) as it:
                for u in range(UNROLL):
                    s, n = slot_of(l, it, u, 0)
                    row = sp.snap((it * UNROLL + u) * P)
                    sp.wait_ge(y_ready[s], n + 1)
                    sp.dma_start(y_dram[l][bass.ds(row, P), :], y_sb[s][:]).then_inc(y_stored[s], 16)

        @block.sync
        def _(sp):
            for i in range(TT):
                sp.dma_start(x_sb[:, i, :], x_in[i * P:(i + 1) * P, :]).then_inc(x_loaded[i], 16)
                if i == 1:
                    sp.dma_start(ident_sb[:], ident[:, :]).then_inc(const_in, 16)
                    sp.dma_start(gate_sb[:], gate[:, :, :]).then_inc(const_in, 16)
            sp.dma_start(tri_sb[:], tri[:, :, :]).then_inc(const_in, 16)
            sp.dma_start(iota_sb[:], iotas[:, 0:P]).then_inc(const_in, 16)
            sp.dma_start(tok_sb[:], iotas[:, P:P + TT * TOP_K]).then_inc(const_in, 16)
            sp.dma_start(thr_sb[:], iotas[:, P + TT * TOP_K:]).then_inc(const_in, 16)
            sp.dma_start(scan_keep_sb[:], scan_keep[:, :]).then_inc(const_in, 16)
            for i in range(TT):
                sp.wait_ge(xn_ready, i + 1)
                sp.dma_start(xn_dram[0][i * P:(i + 1) * P, :], xn_sb[:, i, :]).then_inc(xn_stored[0], 16)
                for c in (2 * i, 2 * i + 1):
                    sp.dma_start(w_up_sb[:, c * CHUNK_BYTES_COLS:(c + 1) * CHUNK_BYTES_COLS],
                                 w_up[c, :, :]).then_inc(w_in[c], 16)
                    sp.dma_start(w_down_sb[:, c * 2 * D:(c + 1) * 2 * D], w_down[c, :, :]).then_inc(w_in[c], 16)
            for c in range(NCH):
                sp.wait_ge(w_in[c], 32)
                sp.sem_inc(w_ready, 1)
            store_results(sp, 0)

            sp.dma_start(cos_sb, cos[:, :]).then_inc(const_in, 16)
            sp.dma_start(sin_sb, sin[:, :]).then_inc(const_in, 16)
            with sp.Fori(0, HKV) as g:
                sp.wait_ge(v_mm, g + 1)
                sp.wait_ge(proj_mm, g * 10 + 1)
                sp.dma_start(wk_sb, wk[bass.ds(g, 1), :, :].rearrange("a p n -> p (a n)")).then_inc(kv_in, 16)
                sp.dma_start(wv_sb, wv[bass.ds(g, 1), :, :].rearrange("a p n -> p (a n)")).then_inc(kv_in, 16)
                for hh in range(GROUPS):
                    u = hh % 2
                    if hh >= 2:
                        sp.wait_ge(proj_mm, g * 10 + 2 * hh + 1)
                    sp.dma_start(wq_sb[u], wq[bass.ds(g * GROUPS + hh, 1), :, :]
                                 .rearrange("a p n -> p (a n)")).then_inc(wq_in[u], 16)
                    sp.wait_ge(masked[1], g * 16 + (4 * (hh - 1) if hh >= 2 else 0) + 1)
                    sp.dma_start(decay_sb[u], decay[bass.ds(g * GROUPS + hh, 1), :, :]
                                 .rearrange("a p n -> p (a n)")).then_inc(decay_in[u], 16)
                    sp.wait_ge(wo_mm[1], g * 4 + (hh - 1 if hh >= 2 else 0) + 1)
                    sp.dma_start(wo_sb[u], wo[bass.ds(g * GROUPS + hh, 1), :, :]
                                 .rearrange("a p n -> p (a n)")).then_inc(wo_in[u], 16)

            for i in range(TT):
                sp.wait_ge(xn_ready, 2 * TT + i + 1)
                sp.dma_start(xn_dram[1][i * P:(i + 1) * P, :], xn_sb[:, i, :]).then_inc(xn_stored[1], 16)
            store_results(sp, 1)
            for i in range(TT):
                sp.wait_ge(x_done, TT + i + 1)
                sp.dma_start(out[i * P:(i + 1) * P, :], x_sb[:, i, :]).then_inc(out_stored, 16)
            sp.wait_ge(out_stored, 16 * TT)

        def moe_pool(pool, l):
            if l == 0:
                pool.wait_ge(const_in, 16 * 7)
            pool.wait_ge(slots_ready, l + 1)
            NP_ = TT * TOP_K
            nc.gpsimd.tensor_tensor(hot_q, hot_q, tok_sb[:].unsqueeze(2).broadcast_to([P, NP_, SLOT_TILES]),
                                    ALU.mult).then_inc(hot_q_ready, 1)
            pool.wait_ge(xn_stored[l], 16 * TT)
            pool.wait_ge(ids_ready, l + 1)
            with pool.Fori(0, ROUNDS) as it:
                for u in range(UNROLL):
                    s, n = slot_of(l, it, u, 0, XG)
                    pool.wait_ge(xg_used[s], n)
                    pool.sem_inc(waits_passed, 1)
                    nc.gpsimd.tensor_copy(ids_col[s][:], ids[:, bass.ds(it * UNROLL + u, 1)]).then_inc(col_ready, 1)
                    pool.wait_ge(col_ready, (it + l * ROUNDS) * UNROLL + (u + 1))
                    pool.sem_inc(waits_passed, 1)
                    pool.indirect_dma_start(out=xg[s], out_offset=None, in_=xn_dram[l][:, :],
                                            in_offset=bass.IndirectOffsetOnAxis(ap=ids_col[s][:, 0:1], axis=0)
                                            ).then_inc(xg_ready[s], 16)

        def combine_pool(pool, l):
            for u in range(2):
                pool.wait_ge(y_stored[u], ((l + 1) * SLOT_TILES // 2 + 1) * 16)
            for n in range(TT * TOP_K):
                uses = l * (TT * TOP_K // YG) + n // YG
                pool.wait_ge(yg_used[n % YG], uses)
                pool.indirect_dma_start(out=yg[n % YG], out_offset=None, in_=y_dram[l][:, :],
                                        in_offset=bass.IndirectOffsetOnAxis(ap=slot_ix[:, n:n + 1], axis=0)
                                        ).then_inc(yg_ready[n % YG], 16)

        @block.gpsimd
        def _(pool):
            for one in (xg_used + xgT_ready + h_mm + silu_ready + act_ready + actT_mm + actT_ready + y_mm + y_ready
                        + [proj_mm, v_mm, scores_done, rope_read, pv_mm, o_copied] + masked + wo_mm + roped):
                pool.sem_inc(one, 1)
            for one in y_stored:
                pool.sem_inc(one, 16)
            moe_pool(pool, 0)
            combine_pool(pool, 0)
            with pool.Fori(0, HKV) as g:
                for j in range(10):
                    pool.wait_ge(rope_read, g * 10 + j + 1 + 1)
                    if j == 0:
                        pool.wait_ge(scores_done, g * 8 + 1)
                    if j >= 3:
                        pool.wait_ge(scores_done, g * 8 + j - 3 + 1)
                    dst = kT[j] if j < 2 else qT[j % 2]
                    nc.gpsimd.tensor_tensor(dst, rope_a[j % 2], rope_b[j % 2], ALU.add).then_inc(roped[j % 2], 1)
            moe_pool(pool, 1)
            combine_pool(pool, 1)

        def norm_act(act_e, s):
            def transposed(i):
                n = s * TT + i
                act_e.wait_ge(xnT_mm, n + 1)
                nc.scalar.activation(xnT[:, :, i * P:(i + 1) * P],
                                     xT_ps[n % 2][:, 0:D].rearrange("p (k t) -> p k t", k=KD), ACT.Copy).then_inc(xnT_copied, 1)
            for i in range(TT):
                n = s * TT + i
                act_e.wait_ge(rvar_ready, n + 1)
                nc.scalar.activation(rstd[:, i:i + 1], rvar[:, i:i + 1], ACT.Sqrt).then_inc(rstd_ready, 1)
                if i >= 1:
                    transposed(i - 1)
            transposed(TT - 1)

        def moe_act(act_e, l):
            norm_act(act_e, 2 * l)
            act_e.wait_ge(logits_mm, (l + 1) * TT)
            nc.scalar.activation(lg[:], logit_ps[:, 0:TT * E].rearrange("p (t e) -> p t e", t=TT), ACT.Copy).then_inc(lg_ready, 1)
            act_e.wait_ge(rel_ready, l + 1)
            nc.scalar.activation(top_exp[:], top_rel[:], ACT.Exp).then_inc(exp_ready, 1)

            def step(it, u, t):
                if t is None or t < SLOT_TILES:
                    s, n = slot_of(l, it, u, 0)
                    act_e.wait_ge(h_mm[s], n + 1)
                    act_e.wait_ge(act_ready[s], n)
                    nc.scalar.activation(silu_g[s], h_ps[s][:, 0:WI], ACT.Silu).then_inc(silu_ready[s], 1)
                if t is None or t >= 2:
                    s, n = slot_of(l, it, u, -2)
                    act_e.wait_ge(y_mm[s], n + 1)
                    act_e.wait_ge(y_stored[s], n * 16)
                    nc.scalar.activation(y_sb[s][:], y_ps[s][:, 0:D], ACT.Copy).then_inc(y_ready[s], 1)
            expert_steps(act_e, step, 0, SLOT_TILES + 2)

        @block.scalar
        def _(act_e):
            moe_act(act_e, 0)
            norm_act(act_e, 1)
            with act_e.Fori(0, HKV) as g:
                act_e.wait_ge(v_mm, g + 1 + 1)
                act_e.wait_ge(pv_mm, g * 8 + 1)
                for b in range(B):
                    nc.scalar.activation(v_sb[:, b * SB:(b + 1) * SB, :],
                                         sc_ps[b][:, :].rearrange("p (t d) -> p t d", t=SB), ACT.Copy).then_inc(v_copied, 1)
                for m in range(8):
                    act_e.wait_ge(pv_mm, g * 8 + m + 1 + 1)
                    act_e.wait_ge(wo_mm[m % 2], g * 4 + m // 2 + 1)
                    nc.scalar.activation(oT[m % 2], o_ps[:, :], ACT.Copy).then_inc(o_copied, 1)
            for u in range(2):
                act_e.wait_ge(wo_mm[u], 4 * HKV + 1)
            for i in range(TT):
                nc.scalar.activation(x_sb[:, i, :], res_ps[i], ACT.Copy).then_inc(x2_copied, 1)
            moe_act(act_e, 1)

        def moments(dve, link, s, i):
            if s == 0:
                dve.wait_ge(x_loaded[i], 16)
            if s == 2:
                dve.wait_ge(x2_copied, i + 1)
            link(nc.vector.bn_stats(stats[:], x_sb[:, i, :]))
            link(nc.vector.bn_aggr(mv[:, i, :], stats[:]))
            link(nc.vector.tensor_scalar_add(var_eps[:, i:i + 1], mv[:, i, 1:2], LN_EPS))
            nc.vector.reciprocal(rvar[:, i:i + 1], var_eps[:, i:i + 1]).then_inc(rvar_ready, 1)

        def normalise(dve, s, i):
            n = s * TT + i
            dve.wait_ge(rstd_ready, n + 1)
            if s == 1 and i == 0:
                dve.wait_ge(xn_stored[0], 16 * TT)
            if s >= 1:
                dve.wait_ge(xnT_mm, (s - 1) * TT + i + 1)
            nc.vector.tensor_scalar(xn_sb[:, i, :], x_sb[:, i, :], mv[:, i, 0:1], rstd[:, i:i + 1],
                                    ALU.subtract, ALU.mult).then_inc(xn_ready, 1)

        def route_dve(dve, link, l):
            NP_ = TT * TOP_K
            if l == 0:
                dve.wait_ge(const_in, 16 * 7)
            dve.wait_ge(lg_ready, l + 1)
            for i in range(TT):
                ins = nc.vector.max(top[:, i, :], lg[:, i, :])
            link(ins)
            for i in range(TT):
                ins = nc.vector.max_index(top_ix[:, i, :], top[:, i, :], lg[:, i, :])
            link(ins)
            link(nc.vector.tensor_copy(ixf[:], top_ix[:, :, 0:TOP_K]))
            link(nc.vector.tensor_tensor(chosen, iota_sb[:, 0:E].unsqueeze(1).unsqueeze(1).broadcast_to([P, TT, TOP_K, E]),
                                         ixf[:].unsqueeze(3).broadcast_to([P, TT, TOP_K, E]), ALU.is_equal))
            with nc.allow_low_precision("zeros and ones"):
                nc.vector.tensor_reduce(member[:], chosen.rearrange("p t k e -> p t e k"), AX.X,
                                        ALU.add).then_inc(member_ready, 1)
            nc.vector.tensor_tensor(top_rel[:], top[:, :, 0:TOP_K], top[:, :, 0:1].broadcast_to([P, TT, TOP_K]),
                                    ALU.subtract).then_inc(rel_ready, 1)
            dve.wait_ge(rank_mm, l + 1)
            link(nc.vector.tensor_copy(tot, tot_ps[:, 0:TT * E].rearrange("p (t e) -> p e t", t=TT)))
            link(nc.vector.tensor_tensor_scan(tot_incl.rearrange("p e t -> p (e t)"), scan_keep_sb[:],
                                              tot.rearrange("p e t -> p (e t)"), 0.0, ALU.mult, ALU.add))
            nc.vector.tensor_tensor(tot_excl, tot_incl, tot, ALU.subtract)
            link(nc.vector.tensor_tensor(over, tot_incl[:, :, TT - 1:TT].broadcast_to([P, E, TT]),
                                         thr_sb[:].unsqueeze(1).broadcast_to([P, E, TT]), ALU.is_gt))
            link(nc.vector.tensor_reduce(ntile[:], over, AX.X, ALU.add))
            link(nc.vector.tensor_tensor_scan(ntile_incl[:], ones_e[:], ntile[:], 0.0, ALU.mult, ALU.add))
            link(nc.vector.tensor_tensor(ntile_excl[:], ntile_incl[:], ntile[:], ALU.subtract))
            link(nc.vector.scalar_tensor_tensor(slot_base[:], ntile_excl[:].unsqueeze(2).broadcast_to([P, E, TT]), float(P),
                                                tot_excl, ALU.mult, ALU.add))
            link(nc.vector.tensor_tensor(slot_te[:], rank_ps[:, 0:TT * E].rearrange("p (t e) -> p t e", t=TT),
                                         slot_base[:].rearrange("p e t -> p t e"), ALU.add))
            link(nc.vector.tensor_tensor(slot_pick, chosen, slot_te[:].unsqueeze(2).broadcast_to([P, TT, TOP_K, E]),
                                         ALU.mult))
            link(nc.vector.tensor_reduce(slotf[:], slot_pick.rearrange("p t k e -> p (t k) e"), AX.X, ALU.add))
            link(nc.vector.tensor_copy(slot_ix[:], slotf[:]))
            nc.vector.tensor_single_scalar(slot_qi[:], slot_ix[:], 7, ALU.arith_shift_right)
            link(nc.vector.tensor_single_scalar(slot_ri[:], slot_ix[:], P - 1, ALU.bitwise_and))
            nc.vector.tensor_copy(slot_q[:], slot_qi[:])
            link(nc.vector.tensor_copy(slot_r[:], slot_ri[:]))
            nc.vector.tensor_tensor(hot_q, iota_sb[:, 0:SLOT_TILES].unsqueeze(1).broadcast_to([P, NP_, SLOT_TILES]),
                                    slot_q[:].unsqueeze(2).broadcast_to([P, NP_, SLOT_TILES]), ALU.is_equal).then_inc(slots_ready, 1)
            nc.vector.tensor_tensor(hot_r, iota_sb[:].unsqueeze(1).broadcast_to([P, NP_, P]),
                                    slot_r[:].unsqueeze(2).broadcast_to([P, NP_, P]), ALU.is_equal).then_inc(hot_r_ready, 1)
            link(nc.vector.tensor_tensor(tile_ge, iota_sb[0:1, 0:SLOT_TILES].unsqueeze(2).broadcast_to([1, SLOT_TILES, E]),
                                         ntile_incl[0:1, :].unsqueeze(1).broadcast_to([1, SLOT_TILES, E]), ALU.is_ge))
            link(nc.vector.tensor_reduce(tile_e[:], tile_ge, AX.X, ALU.add))
            link(nc.vector.tensor_scalar(tile_e_i[:], tile_e[:], float(E - 1), None, ALU.min))
            nc.vector.tensor_single_scalar(tile_c_i[:], tile_e_i[:], 1, ALU.arith_shift_right).then_inc(tiles_ready, 1)
            dve.wait_ge(ids_mm, l + 1)
            nc.vector.tensor_copy(ids[:], ids_ps[:, 0:SLOT_TILES]).then_inc(ids_ready, 1)
            dve.wait_ge(exp_ready, l + 1)
            link(nc.vector.tensor_reduce(top_sum[:], top_exp[:], AX.X, ALU.add))
            link(nc.vector.reciprocal(top_sum[:], top_sum[:]))
            link(nc.vector.scalar_tensor_tensor(wgt[:], top_exp[:], 0.5, top_sum[:].unsqueeze(2).broadcast_to([P, TT, TOP_K]),
                                                ALU.mult, ALU.mult))

        def experts_dve(dve, l):
            def step(it, u, t):
                if t is None or 1 <= t <= SLOT_TILES:
                    s, n = slot_of(l, it, u, -1)
                    dve.wait_ge(actT_mm[s], n + 1)
                    dve.wait_ge(y_mm[s], n)
                    nc.vector.tensor_copy(actT[s][0:MI, 0, :], aT_ps[s][0:MI, 0:P])
                    nc.vector.tensor_copy(actT[s][:, 1, :], aT_ps[s][:, P:2 * P]).then_inc(actT_ready[s], 1)
                if t is None or t < SLOT_TILES - 1:
                    rows_in(it, u, 1)
                if t is None or t < SLOT_TILES:
                    s, n = slot_of(l, it, u, 0)
                    dve.wait_ge(silu_ready[s], n + 1)
                    dve.wait_ge(actT_mm[s], n)
                    nc.vector.tensor_tensor(act[s][:, 0:MI], silu_g[s][:, 0:MI], h_ps[s][:, WI:WI + MI], ALU.mult)
                    nc.vector.scalar_tensor_tensor(act[s][:, MI:WI], silu_g[s][:, MI:WI], SMALL_SCALE,
                                                   h_ps[s][:, WI + MI:2 * WI], ALU.mult, ALU.mult).then_inc(act_ready[s], 1)

            def rows_in(it, u, d):
                g, gn = slot_of(l, it, u, d, XG)
                s, n = slot_of(l, it, u, d)
                dve.wait_ge(xg_used[g], gn + 1)
                dve.wait_ge(h_mm[s], n)
                nc.vector.tensor_copy(xgT[s], xT_ps[s][:, 0:D].rearrange("p (k t) -> p k t", k=KD)).then_inc(xgT_ready[s], 1)

            rows_in(0, 0, 0)
            expert_steps(dve, step, 0, SLOT_TILES + 1)

        def combine(dve, link, l, i):
            for k in range(TOP_K):
                n = i * TOP_K + k
                dve.wait_ge(yg_ready[n % YG], 16 * (l * (TT * TOP_K // YG) + n // YG + 1))
                ins = nc.vector.scalar_tensor_tensor(x_sb[:, i, :], yg[n % YG], wgt[:, i, k:k + 1], x_sb[:, i, :],
                                                     ALU.mult, ALU.add)
                ins.then_inc(yg_used[n % YG], 1)
                dve.wait_ge(yg_used[n % YG], l * (TT * TOP_K // YG) + n // YG + 1)
            dve.sem_inc(x_done, 1)

        def attention_dve(dve):
            dve.wait_ge(const_in, 16 * (7 + 2))

            def rotate(g, j):
                u = j % 2
                dve.wait_ge(proj_mm, g * 10 + j + 1 + 1)
                dve.wait_ge(roped[u], g * 5 + j // 2 + 1)
                h = DH // 2
                nc.vector.tensor_tensor(rope_a[u], proj_ps[:, :], cos_sb, ALU.mult)
                nc.vector.tensor_tensor(rope_b[u][0:h, :], proj_ps[h:DH, :], sin_sb[h:DH, :], ALU.mult)
                nc.vector.tensor_tensor(rope_b[u][h:DH, :], proj_ps[0:h, :], sin_sb[0:h, :], ALU.mult).then_inc(rope_read, 1)

            def mask(g, m, j):
                hu = (m // 2) % 2
                if j == 0:
                    dve.wait_ge(pv_mm, g * 8 + m + 1)
                    dve.wait_ge(decay_in[hu], (g * 2 + m // 4) * 16 + 16)
                dve.wait_ge(scores_mm, (g * 8 + m) * SB + j + 1)
                nc.vector.tensor_tensor(probs[j], sc_ps[j % 2][:, 0:S - j * P], decay_sb[hu][:, 0:S - j * P],
                                        ALU.mult).then_inc(masked[j % 2], 1)

            with dve.Fori(0, HKV) as g:
                rotate(g, 0)
                rotate(g, 1)
                rotate(g, 2)
                for m in range(8):
                    mask(g, m, 0)
                    mask(g, m, 1)
                    if m < 7:
                        rotate(g, m + 3)
                    mask(g, m, 2)
                    mask(g, m, 3)

        @block.vector
        def _(dve):
            chain = [0]

            def link(ins):
                chain[0] += 1
                ins.then_inc(dve_step, 1)
                dve.wait_ge(dve_step, chain[0])

            link(nc.vector.memset(ones_e[:], 1.0))
            for i in range(TT):
                if i == 0:
                    dve.wait_ge(x_loaded[0], 16)
                moments(dve, link, 0, i)
                if i >= 1:
                    normalise(dve, 0, i - 1)
            normalise(dve, 0, TT - 1)
            route_dve(dve, link, 0)
            experts_dve(dve, 0)
            for i in range(TT):
                combine(dve, link, 0, i)
                moments(dve, link, 1, i)
                if i >= 1:
                    normalise(dve, 1, i - 1)
            normalise(dve, 1, TT - 1)
            attention_dve(dve)
            for i in range(TT):
                moments(dve, link, 2, i)
                if i >= 1:
                    normalise(dve, 2, i - 1)
            normalise(dve, 2, TT - 1)
            route_dve(dve, link, 1)
            experts_dve(dve, 1)
            for i in range(TT):
                combine(dve, link, 1, i)

        def transpose_rows(pe, s, after=None):
            for i in range(TT):
                n = s * TT + i
                pe.wait_ge(xn_ready, n + 1)
                if n >= 2:
                    pe.wait_ge(xnT_copied, n - 1)
                for k in range(KD):
                    ins = nc.tensor.transpose(xT_ps[n % 2][:, k * P:(k + 1) * P], xn_sb[:, i, k * P:(k + 1) * P], ident_sb[:])
                ins.then_inc(xnT_mm, 1)
                if after and i >= 1:
                    after(i - 1)
            if after:
                after(TT - 1)

        def moe_pe(pe, l):
            def logits(i):
                pe.wait_ge(xnT_copied, 2 * l * TT + i + 1)
                for k in range(KD):
                    ins = nc.tensor.matmul(logit_ps[:, i * E:(i + 1) * E], xnT[:, k, i * P:(i + 1) * P], gate_sb[:, k, :],
                                           start=(k == 0), stop=(k == KD - 1))
                ins.then_inc(logits_mm, 1)
            transpose_rows(pe, 2 * l, logits)
            pe.wait_ge(member_ready, l + 1)
            mem = member[:].rearrange("p t e -> p (t e)")
            nc.tensor.matmul(rank_ps[:, 0:TT * E], tri_sb[:, 0, :], mem, start=True, stop=True)
            nc.tensor.matmul(tot_ps[:, 0:TT * E], tri_sb[:, 1, :], mem, start=True, stop=True).then_inc(rank_mm, 1)
            pe.wait_ge(hot_q_ready, l + 1)
            pe.wait_ge(hot_r_ready, l + 1)
            NP_ = TT * TOP_K
            for n in range(NP_):
                ins = nc.tensor.matmul(ids_ps[:, 0:SLOT_TILES], hot_r[:, n, :], hot_q[:, n, :], start=(n == 0), stop=(n == NP_ - 1))
            ins.then_inc(ids_mm, 1)

            pe.wait_ge(tiles_ready, l + 1)
            pe.wait_ge(ids_ready, l + 1)

            def rows_T(it, u, d):
                g, gn = slot_of(l, it, u, d, XG)
                s, n = slot_of(l, it, u, d)
                pe.wait_ge(xg_ready[g], gn * 16)
                pe.wait_ge(xgT_ready[s], n)
                for k in range(KD):
                    ins = nc.tensor.transpose(xT_ps[s][:, k * P:(k + 1) * P], xg[g][:, k * P:(k + 1) * P], ident_sb[:])
                ins.then_inc(xg_used[g], 1)

            def up(it, u):
                s, n = slot_of(l, it, u, 0)
                t = it * UNROLL + u
                e = pe.value_load(tile_e_i[0:1, bass.ds(t, 1)], min_val=0, max_val=E - 1)
                c = pe.value_load(tile_c_i[0:1, bass.ds(t, 1)], min_val=0, max_val=NCH - 1)
                if l == 0:
                    pe.wait_ge(w_ready, c + 1)
                pe.wait_ge(xgT_ready[s], n + 1)
                pe.wait_ge(act_ready[s], n)
                h2 = h_ps[s][:, 0:2 * WI].rearrange("p (a n) -> p a n", a=2)
                for k in range(KD):
                    w = w_up_sb[:, bass.ds(c * (CHUNK_BYTES_COLS - EXP_COLS) + e * (2 * MI) + k * EXP_COLS, 2 * MI)]
                    nc.tensor.matmul(h2[:, :, 0:MI], xgT[s][:, k, :], w.rearrange("p (a n) -> p a n", a=2), start=(k == 0), stop=(k == KD - 1))
                for k in range(KD):
                    w = w_up_sb[:, bass.ds(c * CHUNK_BYTES_COLS + (KD * EXP_COLS + k * CH_COLS), CH_COLS)]
                    ins = nc.tensor.matmul(h2[:, :, MI:WI], xgT[s][:, k, :], w.rearrange("p (a n) -> p a n", a=2), start=(k == 0), stop=(k == KD - 1))
                ins.then_inc(h_mm[s], 1)

            def act_T(it, u):
                s, n = slot_of(l, it, u, -1)
                pe.wait_ge(act_ready[s], n + 1)
                pe.wait_ge(actT_ready[s], n)
                nc.tensor.transpose(aT_ps[s][0:MI, 0:P], act[s][:, 0:MI], ident_sb[:])
                nc.tensor.transpose(aT_ps[s][:, P:2 * P], act[s][:, MI:WI], ident_sb[:]).then_inc(actT_mm[s], 1)

            def down(it, u):
                s, n = slot_of(l, it, u, -2)
                t = it * UNROLL + u - 2
                e = pe.value_load(tile_e_i[0:1, bass.ds(t, 1)], min_val=0, max_val=E - 1)
                c = pe.value_load(tile_c_i[0:1, bass.ds(t, 1)], min_val=0, max_val=NCH - 1)
                pe.wait_ge(actT_ready[s], n + 1)
                pe.wait_ge(y_ready[s], n)
                nc.tensor.matmul(y_ps[s][:, 0:D], actT[s][0:MI, 0, :], w_down_sb[:, bass.ds(e * D, D)], start=True, stop=False)
                nc.tensor.matmul(y_ps[s][:, 0:D], actT[s][:, 1, :],
                                 w_up_sb[:, bass.ds(c * CHUNK_BYTES_COLS + (KD * EXP_COLS + KD * CH_COLS), D)],
                                 start=False, stop=True).then_inc(y_mm[s], 1)

            def step(it, u, t):
                if t is None or t < SLOT_TILES:
                    up(it, u)
                if t is None or 1 <= t <= SLOT_TILES:
                    act_T(it, u)
                if t is None or t < SLOT_TILES - 1:
                    rows_T(it, u, 1)
                if t is None or t >= 2:
                    down(it, u)

            rows_T(0, 0, 0)
            expert_steps(pe, step, 0, SLOT_TILES + 2)

        def attention_pe(pe):
            def project(g, j):
                m = j - 2
                b = j % 2
                if j == 0:
                    pe.wait_ge(kv_in, g * 32 + 32)
                if j >= 2 and b == 0:
                    pe.wait_ge(wq_in[(m // 2) % 2], (g * 2 + m // 4) * 16 + 16)
                w = wk_sb if j < 2 else wq_sb[(m // 2) % 2]
                pe.wait_ge(rope_read, g * 10 + j + 1)
                for k in range(KD):
                    ins = nc.tensor.matmul(proj_ps[:, :], w[:, k, :], xnT[:, k, b * S:(b + 1) * S], start=(k == 0), stop=(k == KD - 1))
                ins.then_inc(proj_mm, 1)

            def values(g):
                for b in range(B):
                    pe.wait_ge(masked[b], g * 16 + 1)
                    for t in range(SB):
                        for k in range(KD):
                            i = b * SB + t
                            ins = nc.tensor.matmul(sc_ps[b][:, t * DH:(t + 1) * DH], xnT[:, k, i * P:(i + 1) * P],
                                                   wv_sb[:, k, :], start=(k == 0), stop=(k == KD - 1))
                ins.then_inc(v_mm, 1)

            def scores(g, m, j):
                if j == 0:
                    q = m + 2
                    if m == 0:
                        pe.wait_ge(v_copied, g * 2 + 2)
                        pe.wait_ge(roped[1], g * 5 + 1 + 1)
                    pe.wait_ge(roped[q % 2], g * 5 + q // 2 + 1 + 1)
                pe.wait_ge(masked[j % 2], (g * 8 + m) * 2 + j // 2 + 1)
                ins = nc.tensor.matmul(sc_ps[j % 2][:, 0:S - j * P], kT[m % 2][:, j * P:(j + 1) * P], qT[m % 2][:, j * P:],
                                       start=True, stop=True)
                ins.then_inc(scores_mm, 1)

            def products(g, m):
                pe.wait_ge(o_copied, g * 8 + m + 1)
                for j in range(SB):
                    pe.wait_ge(masked[j % 2], (g * 8 + m) * 2 + j // 2 + 1 + 1)
                    ins = nc.tensor.matmul(o_ps[:, j * P:], v_sb[:, (m % 2) * SB + j, :], probs[j], start=(j == 0), stop=(j == SB - 1),
                                           skip_group_check=True)
                ins.then_inc(pv_mm, 1)

            def output(g, m):
                hu = (m // 2) % 2
                pe.wait_ge(wo_in[hu], (g * 2 + m // 4) * 16 + 16)
                pe.wait_ge(o_copied, g * 8 + m + 1 + 1)
                for t in range(SB):
                    ins = nc.tensor.matmul(res_ps[(m % 2) * SB + t], oT[m % 2][:, t * P:(t + 1) * P], wo_sb[hu], start=False, stop=False,
                                           skip_group_check=True)
                ins.then_inc(wo_mm[m % 2], 1)

            pe.wait_ge(x_done, TT)
            for i in range(0, TT, 2):
                nc.tensor.matmul(bank[4 + i // 2][:, :], ident_sb[:], x_sb[:, i:i + 2, :], start=True, stop=False, skip_group_check=True)
            pe.wait_ge(xnT_copied, 2 * TT)
            with pe.Fori(0, HKV) as g:
                project(g, 0)
                project(g, 1)
                values(g)
                project(g, 2)
                for m in range(8):
                    scores(g, m, 0)
                    scores(g, m, 1)
                    if m < 7:
                        project(g, m + 3)
                    scores(g, m, 2)
                    scores(g, m, 3)
                    pe.wait_ge(scores_mm, (g * 8 + m) * SB + SB)
                    pe.sem_inc(scores_done, 1)
                    if m >= 1:
                        output(g, m - 1)
                    products(g, m)
                output(g, 7)

        @block.tensor
        def _(pe):
            pe.wait_ge(const_in, 16 * 7)
            moe_pe(pe, 0)
            transpose_rows(pe, 1)
            attention_pe(pe)
            moe_pe(pe, 1)


def _constants():
    f = np.float32
    half = np.arange(0, DH, 2, dtype=f) / f(DH)
    inv_freq = (f(1.0) / np.power(f(10000.0), half)).astype(f)
    ang = np.arange(S, dtype=f)[:, None] * inv_freq[None, :]
    c, s = np.cos(ang).astype(f).T, np.sin(ang).astype(f).T
    cos = np.concatenate([c, c], 0)
    sin = np.concatenate([s, -s], 0)
    lam = np.exp2(-8.0 * np.arange(1, H + 1, dtype=f) / f(H)).astype(f)
    diff = np.arange(S, dtype=f)[None, :] - np.arange(P, dtype=f)[:, None]
    decay = np.where(diff[None] >= 0, np.exp(-lam[:, None, None] * np.maximum(diff, 0)[None]), 0.0).astype(f)
    ident = np.eye(P, dtype=f)
    tri = np.stack([np.triu(np.ones((P, P)), 1), np.ones((P, P))], 1).astype(np.float16)
    tok = np.arange(P)[:, None] + P * np.repeat(np.arange(TT), TOP_K)[None, :]
    iotas = np.concatenate([np.tile(np.arange(P), (P, 1)), tok, np.tile(P * np.arange(TT), (P, 1))], 1).astype(f)
    keep = np.tile(np.tile(np.r_[0.0, np.ones(TT - 1)], E), (P, 1)).astype(f)
    return dict(decay=decay, cos=cos, sin=sin, ident=ident, tri=tri, iotas=iotas, scan_keep=keep)


def kernel(L0_attn_x, L0_attn_wq, L0_attn_wk, L0_attn_wv, L0_attn_wo, L0_ffn_gate_w, L0_ffn_Wg, L0_ffn_Wu, L0_ffn_Wd,
           L0_ffn_cWg, L0_ffn_cWu, L0_ffn_cWd):
    import concourse.bacc as _bacc
    from concourse import mybir as _mybir
    from concourse.bass_utils import run_bass_kernel_spmd as _run

    def contract_first(w, heads):
        w = np.asarray(w)
        return w.reshape(heads, -1, KD, P).transpose(0, 3, 2, 1).reshape(heads, P, -1)

    wg, wu, wd = np.asarray(L0_ffn_Wg), np.asarray(L0_ffn_Wu), np.asarray(L0_ffn_Wd)
    cg, cu, cd = np.asarray(L0_ffn_cWg), np.asarray(L0_ffn_cWu), np.asarray(L0_ffn_cWd)
    up = np.stack([wg, wu], 2).reshape(NCH, 2, KD, P, 2 * MI).transpose(0, 3, 2, 1, 4).reshape(NCH, P, -1)
    cup = np.stack([cg, cu], 2).reshape(NCH, KD, P, 2 * CI).transpose(0, 2, 1, 3).reshape(NCH, P, -1)
    arrays = dict(
        x_in=np.asarray(L0_attn_x).reshape(T, D),
        gate=np.asarray(L0_ffn_gate_w).reshape(E, KD, P).transpose(2, 1, 0),
        w_up=np.concatenate([up, cup, cd], 2),
        w_down=wd.reshape(NCH, 2, MI, D).transpose(0, 2, 1, 3).reshape(NCH, MI, 2 * D),
        wq=contract_first(L0_attn_wq, H), wk=contract_first(L0_attn_wk, HKV), wv=contract_first(L0_attn_wv, HKV),
        wo=np.asarray(L0_attn_wo).reshape(D, H, DH).transpose(1, 2, 0),
        **_constants())
    nc = _bacc.Bacc("TRN2", target_bir_lowering=False, num_devices=1)
    args = {}
    for name, a in arrays.items():
        arrays[name] = a = np.ascontiguousarray(a)
        args[name] = nc.dram_tensor(name, a.shape, _mybir.dt.from_np(a.dtype), kind="ExternalInput").ap()
    args["out"] = nc.dram_tensor("out", (T, D), _mybir.dt.float32, kind="ExternalOutput").ap()
    macaron_kernel(nc, **args)
    r = _run(nc, [arrays], core_ids=[0])
    return r.results[0]["out"].reshape(B, S, D)
```

```python
import numpy as np
import concourse.bass as bass
from concourse import mybir
from contextlib import ExitStack

P = 128
B, S, D = 2, 512, 256
T = B * S
TT = T // P
SB = S // P
KD = D // P
H, HKV, DH = 16, 4, 128
GROUPS = H // HKV
E, TOP_K, MI = 32, 4, 96
NCH, CI = 16, 128
SMALL_SCALE = 0.05
EPS = 1e-5
PAIRS = TT * TOP_K
SLOT_TILES = PAIRS + E - 1
MIN_TILES = T * TOP_K // P
GROUP = 2
QW = SLOT_TILES + 1
LOAD = 4
XG, YB, ZB = 4, 4, 4
LAG = 8
WI = MI + CI
EXP_COLS = KD * 2 * MI
CH_COLS = KD * 2 * CI + D
LN_EPS = EPS


def macaron_kernel(nc, x_in, gate, w_exp, w_ch, w_down, wq, wk, wv, wo, decay, cos, sin, ident, tri, iotas, iota16, scan_keep, out):
    f32, f16, i32, u32 = mybir.dt.float32, mybir.dt.float16, mybir.dt.int32, mybir.dt.uint32
    ALU = mybir.AluOpType
    ACT = mybir.ActivationFunctionType
    AX = mybir.AxisListType

    ctx = ExitStack()
    with ctx:
        def sb(name, shape, dt=f32):
            return ctx.enter_context(nc.sbuf_tensor(name, shape, dt))

        def sem(name):
            return ctx.enter_context(nc.semaphore(name))

        def sems(name, n):
            return [sem(f"{name}{i}") for i in range(n)]

        xn_dram = [nc.dram_tensor(f"xn_dram{l}", (T, D), f32).ap() for l in range(2)]
        z_dram = [nc.dram_tensor(f"z_dram{l}", ((T * TOP_K + SLOT_TILES * P), D), f32).ap() for l in range(2)]

        w_exp_sb = sb("w_exp_sb", [P, E * EXP_COLS])
        w_ch_sb = sb("w_ch_sb", [P, NCH * CH_COLS])
        w_down_sb = sb("w_down_sb", [MI, E * D])
        gate_sb = sb("gate_sb", [P, KD, E])
        x_sb = sb("x_sb", [P, TT, D])
        xn_sb = sb("xn_sb", [P, TT, D])
        xnT = sb("xnT", [P, KD, T])
        ident_sb = sb("ident_sb", [P, P])
        tri_sb = sb("tri_sb", [P, 2, P], f16)
        iotas_sb = sb("iotas_sb", [P, E + TT + TT + TOP_K + 1 + QW])
        iota_e = iotas_sb[:, 0:E]
        thr_sb = iotas_sb[:, E:E + TT]
        tok1 = iotas_sb[:, E + TT:E + 2 * TT]
        iota_k = iotas_sb[:, E + 2 * TT:E + 2 * TT + TOP_K]
        part = iotas_sb[:, E + 2 * TT + TOP_K:][:, 0:1]
        dump = iotas_sb[:, E + 2 * TT + TOP_K + 1:]
        iota16_sb = sb("iota16_sb", [P, P], f16)
        scan_keep_sb = sb("scan_keep_sb", [P, E * TT])
        stats = sb("stats", [P, 6])
        mv = sb("mv", [P, TT, 2])
        var_eps = sb("var_eps", [P, TT])
        rvar = sb("rvar", [P, TT])
        rstd = sb("rstd", [P, TT])

        top = sb("top", [P, TT, 8])
        top_ix = sb("top_ix", [P, TT, 8], u32)
        ixf = sb("ixf", [P, TT, TOP_K])
        member2 = sb("member2", [P, 2, TT, E], f16)
        member = sb("member", [P, TT, E], f16)
        top_rel = sb("top_rel", [P, TT, TOP_K])
        top_exp = sb("top_exp", [P, TT, TOP_K])
        top_sum = sb("top_sum", [P, TT])
        wgt = sb("wgt", [P, TT, TOP_K])
        ntile = sb("ntile", [P, E])
        ntile_incl = sb("ntile_incl", [P, E])
        ntile_excl = sb("ntile_excl", [P, E])
        ones_e = sb("ones_e", [P, E])
        slot_base = sb("slot_base", [P, E, TT])
        slot_te = sb("slot_te", [P, TT, E])
        slotf = sb("slotf", [P, TT * TOP_K])
        slot_ix = sb("slot_ix", [P, TT * TOP_K], i32)
        slot_qi = sb("slot_qi", [P, TT * TOP_K], i32)
        slot_ri = sb("slot_ri", [P, TT * TOP_K], i32)
        slot_q = sb("slot_q", [P, TT * TOP_K])
        slot_r = sb("slot_r", [P, TT * TOP_K])
        n_used = sb("n_used", [1, 1], i32)
        tile_ge = sb("tile_ge", [QW, E])
        tile_e = sb("tile_e", [QW, 1])
        tile_ec = sb("tile_ec", [1, 2, QW], i32)
        ids = sb("ids", [P, QW], i32)
        ids_sum = sb("ids_sum", [P, QW])
        dest_k = sb("dest_k", [P, QW])
        dest_empty = sb("dest_empty", [P, QW])
        dest = sb("dest", [P, QW], i32)


        rot = sb("rot", [P, 2, S])
        cos_sb, sin_sb = rot[:, 0, :], rot[:, 1, :]
        wkv_sb = sb("wkv_sb", [P, 2, KD, DH])
        wk_sb, wv_sb = wkv_sb[:, 0, :, :], wkv_sb[:, 1, :, :]
        wq_all = sb("wq_all", [P, 2, KD, DH])
        wq_sb = [wq_all[:, u, :, :] for u in range(2)]
        wo_all = sb("wo_all", [P, 2, D])
        wo_sb = [wo_all[:, u, :] for u in range(2)]
        decay_all = sb("decay_all", [P, 2, S])
        decay_sb = [decay_all[:, u, :] for u in range(2)]
        rope = sb("rope", [P, 4, S])
        rope_a, rope_b = [rope[:, u, :] for u in range(2)], [rope[:, 2 + u, :] for u in range(2)]
        kqT = sb("kqT", [P, 4, S])
        v_all = sb("v_all", [P, TT * DH])
        xn_flat = xn_sb[:, :, :].rearrange("p t d -> p (t d)")
        kT = [[kqT[:, b, :] for b in range(B)], [xn_flat[:, b * S:(b + 1) * S] for b in range(B)]]
        qT = [kqT[:, 2 + u, :] for u in range(2)]
        v_sb = [v_all[:, :].rearrange("p (t d) -> p t d", t=TT),
                xn_flat[:, B * S:2 * B * S].rearrange("p (t d) -> p t d", t=TT)]
        probs_all = sb("probs_all", [P, SB * (SB + 1) // 2 * P])
        probs = [probs_all[:, j * S - j * (j - 1) // 2 * P:(j + 1) * S - (j + 1) * j // 2 * P] for j in range(SB)]
        oT_all = sb("oT_all", [P, 2 * S])
        oT = [oT_all[:, u * S:(u + 1) * S] for u in range(2)]
        chosen = probs_all[:, 0:TT * TOP_K * E].rearrange("p (t k e) -> p t k e", t=TT, k=TOP_K)
        tot, over = [wo_all[:, a, :].rearrange("p (e t) -> p e t", t=TT) for a in range(2)]
        tot_incl, tot_excl = [wq_all[:, a, :, :].rearrange("p k n -> p (k n)").rearrange("p (e t) -> p e t", t=TT)
                              for a in range(2)]
        xg = [decay_all[:, u // 2, (u % 2) * D:(u % 2 + 1) * D] for u in range(XG)]
        xgT = [oT_all[:, u * D:(u + 1) * D].rearrange("p (k t) -> p k t", k=KD) for u in range(2)]
        silu_g = [rot[:, 0, u * WI:(u + 1) * WI] for u in range(2)]
        act = [rot[:, 1, u * WI:(u + 1) * WI] for u in range(2)]
        actT = [wkv_sb[:, u, :, :] for u in range(2)]
        y_sb = [probs_all[:, u * D:(u + 1) * D] for u in range(YB)]
        z_sb = [(kqT if u < 2 else rope)[:, 2 * (u % 2):2 * (u % 2) + 2, :].rearrange("p a (h d) -> p (a h) d", d=D)
                for u in range(ZB)]
        hot_r = rope[:, :, :].rearrange("p a s -> p (a s)").bitcast(f16).rearrange("p (n r) -> p n r", r=P)
        hot_q = v_all[:, :].bitcast(f16).rearrange("p (n q) -> p n q", q=QW)
        slot_pick = oT_all[:, :].rearrange("p (t k e) -> p t k e", t=TT, k=TOP_K)
        dest_hot = kqT[:, 0, 0:TOP_K * QW].rearrange("p (k q) -> p k q", q=QW)

        bank = [ctx.enter_context(nc.psum_tensor(f"bank{i}", [P, 512], f32)) for i in range(8)]
        xT_ps = [bank[0], bank[1]]
        logit_ps = [bank[2 + i % 6] for i in range(TT)]
        rank_ps, tot_ps, ids_ps, tile_ps = bank[3], bank[4], bank[5], bank[6]
        h_ps, aT_ps, y_ps = [bank[2], bank[3]], [bank[4], bank[5]], [bank[6], bank[7]]
        proj_ps, o_ps, sc_ps = bank[0], bank[1], [bank[2], bank[3]]
        res_ps = [bank[4 + i // 2][:, (i % 2) * D:(i % 2 + 1) * D] for i in range(TT)]

        const_in = sem("const_in")
        x_loaded = sems("x_loaded", TT)
        w_in = sems("w_in", NCH)
        dve_step = sem("dve_step")
        rvar_ready, rstd_ready = sem("rvar_ready"), sem("rstd_ready")
        xn_ready, xnT_mm, xnT_copied = sem("xn_ready"), sem("xnT_mm"), sem("xnT_copied")
        xn_stored = sems("xn_stored", 2)
        logits_mm = sem("logits_mm")
        top_ready, index_ready, rel_ready, exp_ready = sem("top_ready"), sem("index_ready"), sem("rel_ready"), sem("exp_ready")
        member_ready, rank_mm = sem("member_ready"), sem("rank_mm")
        used_ready = sem("used_ready")
        hot_ready, tile_e_ready, tile_e_mm = sem("hot_ready"), sem("tile_e_ready"), sem("tile_e_mm")
        ids_mm, ids_ready, tiles_ready, dest_ready = sem("ids_mm"), sem("ids_ready"), sem("tiles_ready"), sem("dest_ready")
        w_ready = sem("w_ready")
        xg_used = sems("xg_used", XG)
        xg_ready = [sems(f"xg_ready{l}_", XG) for l in range(2)]
        y_scattered = [sems(f"y_scattered{l}_", YB) for l in range(2)]
        results_stored = sem("results_stored")
        xgT_ready = sems("xgT_ready", 2)
        h_mm, silu_ready, act_ready = sems("h_mm", 2), sems("silu_ready", 2), sems("act_ready", 2)
        actT_mm, actT_ready = sems("actT_mm", 2), sems("actT_ready", 2)
        y_mm, y_copied = sems("y_mm", 2), sem("y_copied")
        z_in, z_used = sems("z_in", ZB), sem("z_used")
        x_done = sem("x_done")
        out_stored = sem("out_stored")
        kv_in, wq_in, wo_in, decay_in = sem("kv_in"), sems("wq_in", 2), sems("wo_in", 2), sems("decay_in", 2)
        v_copied = sem("v_copied")
        proj_mm, rope_read, roped = sem("proj_mm"), sem("rope_read"), sem("roped")
        scores_mm, masked = sem("scores_mm"), sems("masked", 2)
        pv_mm, o_copied, wo_mm = sem("pv_mm"), sem("o_copied"), sem("wo_mm")
        x2_copied = sem("x2_copied")

        N_CONST = 6

        def slot_of(l, t, buffers=2):
            n = l * SLOT_TILES + t
            return n % buffers, n // buffers

        def uses(l, t, s, buffers):
            return (l * SLOT_TILES + t - s + buffers - 1) // buffers

        def skip(eng, l, t, rings):
            for ring in rings:
                for s, signal in enumerate(ring):
                    eng.wait_ge(signal, uses(l, t, s, len(ring)))
                    left = uses(l + 1, 0, s, len(ring)) - uses(l, t, s, len(ring))
                    if left:
                        eng.sem_inc(signal, left)

        def tiles_used(eng, l):
            eng.wait_ge(used_ready, l + 1)
            return eng.value_load(n_used[0:1, 0:1], min_val=MIN_TILES, max_val=SLOT_TILES)

        def grouped(eng, used, tiles, drain, t=MIN_TILES):
            if t >= SLOT_TILES:
                drain(SLOT_TILES)
                return
            end = min(t + GROUP, SLOT_TILES)
            with eng.If(used > t):
                tiles(t, end)
                grouped(eng, used, tiles, drain, end)
            with eng.Else():
                drain(t)

        UNITS, GU = H * B, GROUPS * B

        def projections(n, place):
            g, m = n // GU, n % GU
            if n < 0:
                return [("k", 0, b) for b in range(B)] + [("v", 0, b) for b in range(B)] + [("q", 0, 0)]
            if place == "scores":
                return [("q", n + 1, (n + 1) % B)] if n + 1 < UNITS else []
            if g + 1 < HKV and 2 <= m < 6:
                return [("v" if m < 4 else "k", g + 1, m % 2)]
            return []

        order = projections(-1, None)
        for n in range(UNITS):
            order += projections(n, "scores") + projections(n, "behind")
        rotated = [p for p in order if p[0] != "v"]
        copied = [p for p in order if p[0] == "v"]

        block = ctx.enter_context(nc.Block())

        def load_results(sp, l):
            sp.wait_ge(results_stored, l + 1)
            for i in range(TT):
                n = l * TT + i
                if n >= ZB:
                    sp.wait_ge(z_used, n - ZB + 1)
                sp.dma_start(z_sb[n % ZB], z_dram[l][i * P * TOP_K:(i + 1) * P * TOP_K, :]
                             .rearrange("(p k) d -> p k d", k=TOP_K)).then_inc(z_in[n % ZB], 16)

        @block.sync
        def _(sp):
            for i in range(TT):
                sp.dma_start(x_sb[:, i, :], x_in[i * P:(i + 1) * P, :]).then_inc(x_loaded[i], 16)
                if i == 1:
                    sp.dma_start(ident_sb[:], ident[:, :]).then_inc(const_in, 16)
                    sp.dma_start(gate_sb[:], gate[:, :, :]).then_inc(const_in, 16)
            sp.dma_start(tri_sb[:], tri[:, :, :]).then_inc(const_in, 16)
            sp.dma_start(iota16_sb[:], iota16[:, :]).then_inc(const_in, 16)
            sp.dma_start(iotas_sb[:], iotas[:, :]).then_inc(const_in, 16)
            sp.dma_start(scan_keep_sb[:], scan_keep[:, :]).then_inc(const_in, 16)
            for i in range(TT):
                for c in (2 * i, 2 * i + 1):
                    sp.dma_start(w_exp_sb[:, 2 * c * EXP_COLS:2 * (c + 1) * EXP_COLS], w_exp[c, :, :]).then_inc(w_in[c], 16)
                    sp.dma_start(w_ch_sb[:, c * CH_COLS:(c + 1) * CH_COLS], w_ch[c, :, :]).then_inc(w_in[c], 16)
                    sp.dma_start(w_down_sb[:, c * 2 * D:(c + 1) * 2 * D], w_down[c, :, :]).then_inc(w_in[c], 16)
            for c in range(NCH):
                sp.wait_ge(w_in[c], 48)
                sp.sem_inc(w_ready, 1)
            load_results(sp, 0)

            sp.dma_start(cos_sb, cos[:, :]).then_inc(const_in, 16)
            sp.dma_start(sin_sb, sin[:, :]).then_inc(const_in, 16)

            def load_kv(g):
                if g >= 1:
                    sp.wait_ge(proj_mm, max(order.index((kind, g - 1, 1)) for kind in "kv") + 1)
                sp.dma_start(wk_sb, wk[g, :, :]).then_inc(kv_in, 16)
                sp.dma_start(wv_sb, wv[g, :, :]).then_inc(kv_in, 16)

            load_kv(0)
            for h in range(H):
                u = h % 2
                if h >= 2:
                    sp.wait_ge(proj_mm, order.index(("q", 2 * (h - 2) + 1, 1)) + 1)
                sp.dma_start(wq_sb[u], wq[h, :, :]).then_inc(wq_in[u], 16)
                if h >= 2:
                    sp.wait_ge(masked[1], 2 * 2 * (h - 1))
                sp.dma_start(decay_sb[u], decay[h, :, :]).then_inc(decay_in[u], 16)
                if h >= 2:
                    sp.wait_ge(wo_mm, 2 * (h - 1))
                sp.dma_start(wo_sb[u], wo[h, :, :]).then_inc(wo_in[u], 16)
                if h % GROUPS == 1 and h // GROUPS + 1 < HKV:
                    load_kv(h // GROUPS + 1)

            load_results(sp, 1)
            for i in range(TT):
                sp.wait_ge(x_done, TT + i + 1)
                sp.dma_start(out[i * P:(i + 1) * P, :], x_sb[:, i, :]).then_inc(out_stored, 16)
            sp.wait_ge(out_stored, 16 * TT)

        def moe_pool(pool, l):
            pool.wait_ge(xn_stored[l], 16 * TT)
            pool.wait_ge(ids_ready, l + 1)

            def gather(t):
                s, n = slot_of(l, t, XG)
                pool.wait_ge(xg_used[s], n)
                pool.indirect_dma_start(out=xg[s], out_offset=None, in_=xn_dram[l][:, :],
                                        in_offset=bass.IndirectOffsetOnAxis(ap=ids[:, t:t + 1], axis=0)
                                        ).then_inc(xg_ready[l][t % XG], 16)

            def scatter(t):
                s, n = slot_of(l, t, YB)
                if t == 0:
                    pool.wait_ge(dest_ready, l + 1)
                pool.wait_ge(y_copied, l * SLOT_TILES + t + 1)
                pool.indirect_dma_start(out=z_dram[l][:, :],
                                        out_offset=bass.IndirectOffsetOnAxis(ap=dest[:, t:t + 1], axis=0),
                                        in_=y_sb[s], in_offset=None).then_inc(y_scattered[l][t % YB], 16)

            def tiles(a, b):
                for t in range(a, b):
                    gather(t)
                    if t >= LAG:
                        scatter(t - LAG)

            def drain(t):
                for u in range(t - LAG, t):
                    scatter(u)
                for u in range(YB):
                    pool.wait_ge(y_scattered[l][u], 16 * uses(0, t, u, YB))
                pool.sem_inc(results_stored, 1)

            tiles(0, MIN_TILES)
            grouped(pool, tiles_used(pool, l), tiles, drain)

        @block.gpsimd
        def _(pool):
            moe_pool(pool, 0)
            for r, (kind, n, b) in enumerate(rotated):
                pool.wait_ge(rope_read, r + 1)
                if kind == "k":
                    if n >= 2:
                        pool.wait_ge(scores_mm, (n - 1) * GU * SB)
                    dst = kT[n % 2][b]
                else:
                    if n >= 2:
                        pool.wait_ge(scores_mm, (n - 1) * SB)
                    dst = qT[n % 2]
                nc.gpsimd.tensor_tensor(dst, rope_a[r % 2], rope_b[r % 2], ALU.add).then_inc(roped, 1)
            moe_pool(pool, 1)

        def norm_act(act_e, s):
            def transposed(i):
                n = s * TT + i
                if s != 1:
                    act_e.wait_ge(xn_ready, n + 1)
                    act_e.dma_start(xn_dram[s // 2][i * P:(i + 1) * P, :], xn_sb[:, i, :]).then_inc(xn_stored[s // 2], 16)
                act_e.wait_ge(xnT_mm, n + 1)
                nc.scalar.activation(xnT[:, :, i * P:(i + 1) * P],
                                     xT_ps[n % 2][:, 0:D].rearrange("p (k t) -> p k t", k=KD), ACT.Copy).then_inc(xnT_copied, 1)
            for i in range(TT):
                n = s * TT + i
                act_e.wait_ge(rvar_ready, n + 1)
                nc.scalar.activation(rstd[:, i:i + 1], rvar[:, i:i + 1], ACT.Sqrt).then_inc(rstd_ready, 1)
                if i >= 1:
                    transposed(i - 1)
            transposed(TT - 1)

        def moe_act(act_e, l):
            norm_act(act_e, 2 * l)
            act_e.wait_ge(rel_ready, l + 1)
            nc.scalar.activation(top_exp[:], top_rel[:], ACT.Exp).then_inc(exp_ready, 1)

            used = tiles_used(act_e, l)

            def silu(t):
                s, n = slot_of(l, t)
                act_e.wait_ge(h_mm[s], n + 1)
                act_e.wait_ge(act_ready[s], n)
                nc.scalar.activation(silu_g[s], h_ps[s][:, 0:WI], ACT.Silu).then_inc(silu_ready[s], 1)

            def results_out(t):
                s, n = slot_of(l, t)
                act_e.wait_ge(y_mm[s], n + 1)
                y, _ = slot_of(l, t, YB)
                if t >= YB:
                    act_e.wait_ge(y_scattered[l][t % YB], t // YB * 16)
                nc.scalar.activation(y_sb[y], y_ps[s][:, 0:D], ACT.Copy).then_inc(y_copied, 1)

            def tiles(a, b):
                for t in range(a, b):
                    silu(t)
                    if t >= 2:
                        results_out(t - 2)

            def drain(t):
                results_out(t - 2)
                results_out(t - 1)
                skip(act_e, l, t, [silu_ready, [y_copied]])

            tiles(0, MIN_TILES)
            grouped(act_e, used, tiles, drain)

        @block.scalar
        def _(act_e):
            moe_act(act_e, 0)
            norm_act(act_e, 1)
            def copy_values(p):
                kind, g, b = p
                if kind == "v":
                    act_e.wait_ge(proj_mm, order.index(p) + 1)
                    if g >= 2:
                        act_e.wait_ge(pv_mm, (g - 1) * GU)
                    nc.scalar.activation(v_sb[g % 2][:, b * SB:(b + 1) * SB, :],
                                         proj_ps[:, :].rearrange("p (t d) -> p t d", t=SB), ACT.Copy).then_inc(v_copied, 1)

            for p in projections(-1, None):
                copy_values(p)
            for n in range(UNITS):
                for p in projections(n, "behind"):
                    copy_values(p)
                act_e.wait_ge(pv_mm, n + 1)
                if n >= 2:
                    act_e.wait_ge(wo_mm, n - 1)
                nc.scalar.activation(oT[n % 2], o_ps[:, :], ACT.Copy).then_inc(o_copied, 1)
            act_e.wait_ge(wo_mm, UNITS)
            for i in range(TT):
                nc.scalar.activation(x_sb[:, i, :], res_ps[i], ACT.Copy).then_inc(x2_copied, 1)
            moe_act(act_e, 1)

        def moments(dve, link, s, i):
            if s == 0:
                dve.wait_ge(x_loaded[i], 16)
            if s == 2:
                dve.wait_ge(x2_copied, i + 1)
            link(nc.vector.bn_stats(stats[:], x_sb[:, i, :]))
            link(nc.vector.bn_aggr(mv[:, i, :], stats[:]))
            link(nc.vector.tensor_scalar_add(var_eps[:, i:i + 1], mv[:, i, 1:2], LN_EPS))
            nc.vector.reciprocal(rvar[:, i:i + 1], var_eps[:, i:i + 1]).then_inc(rvar_ready, 1)

        def normalise(dve, s, i):
            n = s * TT + i
            dve.wait_ge(rstd_ready, n + 1)
            if s == 1 and i == 0:
                dve.wait_ge(xn_stored[0], 16 * TT)
            if s >= 1:
                dve.wait_ge(xnT_mm, (s - 1) * TT + i + 1)
            nc.vector.tensor_scalar(xn_sb[:, i, :], x_sb[:, i, :], mv[:, i, 0:1], rstd[:, i:i + 1],
                                    ALU.subtract, ALU.mult).then_inc(xn_ready, 1)

        def route_dve(dve, link, l):
            if l == 0:
                dve.wait_ge(const_in, 16 * N_CONST)
            for i in range(TT):
                lg = logit_ps[i][:, 0:E]
                dve.wait_ge(logits_mm, l * TT + i + 1)
                nc.vector.max(top[:, i, :], lg).then_inc(top_ready, 1)
                if i >= 1:
                    top_index(dve, l, i - 1)
            top_index(dve, l, TT - 1)
            dve.wait_ge(index_ready, (l + 1) * TT)
            link(nc.vector.tensor_copy(ixf[:], top_ix[:, :, 0:TOP_K]))
            link(nc.vector.tensor_tensor(chosen, iota_e.unsqueeze(1).unsqueeze(1).broadcast_to([P, TT, TOP_K, E]),
                                         ixf[:].unsqueeze(3).broadcast_to([P, TT, TOP_K, E]), ALU.is_equal))
            for a in range(2):
                ins = nc.vector.tensor_tensor(member2[:, a, :, :], chosen[:, :, 2 * a, :], chosen[:, :, 2 * a + 1, :], ALU.add)
            link(ins)
            nc.vector.tensor_tensor(member[:], member2[:, 0, :, :], member2[:, 1, :, :], ALU.add).then_inc(member_ready, 1)
            nc.vector.tensor_tensor(top_rel[:], top[:, :, 0:TOP_K], top[:, :, 0:1].broadcast_to([P, TT, TOP_K]),
                                    ALU.subtract).then_inc(rel_ready, 1)
            dve.wait_ge(rank_mm, l + 1)
            link(nc.vector.tensor_copy(tot, tot_ps[:, 0:TT * E].rearrange("p (t e) -> p e t", t=TT)))
            link(nc.vector.tensor_tensor_scan(tot_incl.rearrange("p e t -> p (e t)"), scan_keep_sb[:],
                                              tot.rearrange("p e t -> p (e t)"), 0.0, ALU.mult, ALU.add))
            nc.vector.tensor_tensor(tot_excl, tot_incl, tot, ALU.subtract)
            link(nc.vector.tensor_tensor(over, tot_incl[:, :, TT - 1:TT].broadcast_to([P, E, TT]),
                                         thr_sb.unsqueeze(1).broadcast_to([P, E, TT]), ALU.is_gt))
            link(nc.vector.tensor_reduce(ntile[:], over, AX.X, ALU.add))
            link(nc.vector.tensor_tensor_scan(ntile_incl[:], ones_e[:], ntile[:], 0.0, ALU.mult, ALU.add))
            nc.vector.tensor_copy(n_used[:], ntile_incl[0:1, E - 1:E]).then_inc(used_ready, 1)
            link(nc.vector.tensor_tensor(ntile_excl[:], ntile_incl[:], ntile[:], ALU.subtract))
            link(nc.vector.scalar_tensor_tensor(slot_base[:], ntile_excl[:].unsqueeze(2).broadcast_to([P, E, TT]), float(P),
                                                tot_excl, ALU.mult, ALU.add))
            link(nc.vector.tensor_tensor(slot_te[:], rank_ps[:, 0:TT * E].rearrange("p (t e) -> p t e", t=TT),
                                         slot_base[:].rearrange("p e t -> p t e"), ALU.add))
            link(nc.vector.tensor_tensor(slot_pick, chosen, slot_te[:].unsqueeze(2).broadcast_to([P, TT, TOP_K, E]),
                                         ALU.mult))
            link(nc.vector.tensor_reduce(slotf[:], slot_pick.rearrange("p t k e -> p (t k) e"), AX.X, ALU.add))
            link(nc.vector.tensor_copy(slot_ix[:], slotf[:]))
            nc.vector.tensor_single_scalar(slot_qi[:], slot_ix[:], 7, ALU.arith_shift_right)
            link(nc.vector.tensor_single_scalar(slot_ri[:], slot_ix[:], P - 1, ALU.bitwise_and))
            nc.vector.tensor_copy(slot_q[:], slot_qi[:])
            link(nc.vector.tensor_copy(slot_r[:], slot_ri[:]))
            for n in [i * TOP_K + k for k in range(TOP_K) for i in range(TT)]:
                nc.vector.tensor_scalar(hot_r[:, n, :], iota16_sb[:], slot_r[:, n:n + 1], None, ALU.is_equal)
                nc.vector.tensor_scalar(hot_q[:, n, :], iota16_sb[:, 0:QW], slot_q[:, n:n + 1], tok1[:, n // TOP_K:n // TOP_K + 1],
                                        ALU.is_equal, ALU.mult).then_inc(hot_ready, 1)
            link(nc.vector.tensor_scalar(tile_ge[:], ntile_incl[0:QW, :], part[0:QW, :], None, ALU.is_le))
            nc.vector.tensor_reduce(tile_e[:], tile_ge[:], AX.X, ALU.add).then_inc(tile_e_ready, 1)
            ids4 = ids_ps[:, 0:TOP_K * QW].rearrange("p (k q) -> p k q", q=QW)
            dve.wait_ge(ids_mm, l + 1)
            link(nc.vector.tensor_reduce(ids_sum[:], ids4.rearrange("p k q -> p q k"), AX.X, ALU.add))
            nc.vector.tensor_scalar(ids[:], ids_sum[:], -1.0, 0.0, ALU.add, ALU.max).then_inc(ids_ready, 1)
            dve.wait_ge(tile_e_mm, l + 1)
            link(nc.vector.tensor_scalar(tile_ec[:, 0, :], tile_ps[0:1, 0:QW], float(E - 1), None, ALU.min))
            nc.vector.tensor_single_scalar(tile_ec[:, 1, :], tile_ec[:, 0, :], 1, ALU.arith_shift_right).then_inc(tiles_ready, 1)
            link(nc.vector.scalar_tensor_tensor(dest_hot, ids4, 0.0, iota_k.unsqueeze(2).broadcast_to([P, TOP_K, QW]),
                                                ALU.is_gt, ALU.mult))
            nc.vector.scalar_tensor_tensor(dest_empty[:], ids_sum[:], 0.0, dump, ALU.is_equal, ALU.mult)
            link(nc.vector.tensor_reduce(dest_k[:], dest_hot.rearrange("p k q -> p q k"), AX.X, ALU.add))
            link(nc.vector.scalar_tensor_tensor(dest_k[:], ids_sum[:], float(TOP_K), dest_k[:], ALU.mult, ALU.add))
            nc.vector.scalar_tensor_tensor(dest[:], dest_k[:], -float(TOP_K), dest_empty[:], ALU.add, ALU.add).then_inc(dest_ready, 1)
            dve.wait_ge(exp_ready, l + 1)
            link(nc.vector.tensor_reduce(top_sum[:], top_exp[:], AX.X, ALU.add))
            link(nc.vector.reciprocal(top_sum[:], top_sum[:]))
            link(nc.vector.scalar_tensor_tensor(wgt[:], top_exp[:], 0.5, top_sum[:].unsqueeze(2).broadcast_to([P, TT, TOP_K]),
                                                ALU.mult, ALU.mult))

        def top_index(dve, l, i):
            dve.wait_ge(top_ready, l * TT + i + 1)
            ins = nc.vector.max_index(top_ix[:, i, :], top[:, i, :], logit_ps[i][:, 0:E])
            ins.then_inc(index_ready, 1)
            return ins

        def experts_dve(dve, l):
            def rows_in(t):
                g, gn = slot_of(l, t, XG)
                s, n = slot_of(l, t)
                dve.wait_ge(xg_used[g], gn + 1)
                dve.wait_ge(h_mm[s], n)
                nc.vector.tensor_copy(xgT[s], xT_ps[s][:, 0:D].rearrange("p (k t) -> p k t", k=KD)).then_inc(xgT_ready[s], 1)

            def hidden_in(t):
                s, n = slot_of(l, t)
                dve.wait_ge(actT_mm[s], n + 1)
                dve.wait_ge(y_mm[s], n)
                nc.vector.tensor_copy(actT[s][0:MI, 0, :], aT_ps[s][0:MI, 0:P])
                nc.vector.tensor_copy(actT[s][:, 1, :], aT_ps[s][:, P:2 * P]).then_inc(actT_ready[s], 1)

            def product(t):
                s, n = slot_of(l, t)
                dve.wait_ge(silu_ready[s], n + 1)
                dve.wait_ge(actT_mm[s], n)
                nc.vector.tensor_tensor(act[s][:, 0:MI], silu_g[s][:, 0:MI], h_ps[s][:, WI:WI + MI], ALU.mult)
                nc.vector.scalar_tensor_tensor(act[s][:, MI:WI], silu_g[s][:, MI:WI], SMALL_SCALE,
                                               h_ps[s][:, WI + MI:2 * WI], ALU.mult, ALU.mult).then_inc(act_ready[s], 1)

            def tiles(a, b):
                for t in range(a, b):
                    rows_in(t)
                    if t >= 1:
                        product(t - 1)
                        hidden_in(t - 1)

            def drain(t):
                product(t - 1)
                hidden_in(t - 1)
                skip(dve, l, t, [xgT_ready, actT_ready, act_ready])

            used = tiles_used(dve, l)
            tiles(0, MIN_TILES)
            grouped(dve, used, tiles, drain)

        def combine(dve, link, l, i):
            n = l * TT + i
            dve.wait_ge(z_in[n % ZB], 16 * (n // ZB + 1))
            for k in range(TOP_K):
                ins = nc.vector.scalar_tensor_tensor(x_sb[:, i, :], z_sb[n % ZB][:, k, :], wgt[:, i, k:k + 1], x_sb[:, i, :],
                                                     ALU.mult, ALU.add)
                if k < TOP_K - 1:
                    link(ins)
            ins.then_inc(z_used, 1)
            dve.wait_ge(z_used, n + 1)
            dve.sem_inc(x_done, 1)

        def attention_dve(dve):
            dve.wait_ge(const_in, 16 * (N_CONST + 2))

            def rotate(p):
                if p[0] == "v":
                    return
                r = rotated.index(p)
                dve.wait_ge(proj_mm, order.index(p) + 1)
                if r >= 2:
                    dve.wait_ge(roped, r - 1)
                h = DH // 2
                nc.vector.tensor_tensor(rope_a[r % 2], proj_ps[:, :], cos_sb, ALU.mult)
                nc.vector.tensor_tensor(rope_b[r % 2][0:h, :], proj_ps[h:DH, :], sin_sb[h:DH, :], ALU.mult)
                nc.vector.tensor_tensor(rope_b[r % 2][h:DH, :], proj_ps[0:h, :], sin_sb[0:h, :], ALU.mult).then_inc(rope_read, 1)

            def mask(n, j):
                h = n // 2
                if j == 0:
                    dve.wait_ge(pv_mm, n)
                    dve.wait_ge(decay_in[h % 2], (h // 2 + 1) * 16)
                dve.wait_ge(scores_mm, n * SB + j + 1)
                nc.vector.tensor_tensor(probs[j], sc_ps[j % 2][:, 0:S - j * P], decay_sb[h % 2][:, 0:S - j * P],
                                        ALU.mult).then_inc(masked[j % 2], 1)

            for p in projections(-1, None):
                rotate(p)
            for n in range(UNITS):
                mask(n, 0)
                mask(n, 1)
                for p in projections(n, "scores"):
                    rotate(p)
                mask(n, 2)
                mask(n, 3)
                for p in projections(n, "behind"):
                    rotate(p)

        @block.vector
        def _(dve):
            chain = [0]

            def link(ins):
                chain[0] += 1
                ins.then_inc(dve_step, 1)
                dve.wait_ge(dve_step, chain[0])

            link(nc.vector.memset(ones_e[:], 1.0))
            for i in range(TT):
                if i == 0:
                    dve.wait_ge(x_loaded[0], 16)
                moments(dve, link, 0, i)
                if i >= 1:
                    normalise(dve, 0, i - 1)
            normalise(dve, 0, TT - 1)
            route_dve(dve, link, 0)
            experts_dve(dve, 0)
            for i in range(TT):
                combine(dve, link, 0, i)
                moments(dve, link, 1, i)
                if i >= 1:
                    normalise(dve, 1, i - 1)
            normalise(dve, 1, TT - 1)
            attention_dve(dve)
            for i in range(TT):
                moments(dve, link, 2, i)
                if i >= 1:
                    normalise(dve, 2, i - 1)
            normalise(dve, 2, TT - 1)
            route_dve(dve, link, 1)
            experts_dve(dve, 1)
            for i in range(TT):
                combine(dve, link, 1, i)

        def transpose_rows(pe, s, after=None):
            for i in range(TT):
                n = s * TT + i
                pe.wait_ge(xn_ready, n + 1)
                if n >= 2:
                    pe.wait_ge(xnT_copied, n - 1)
                for k in range(KD):
                    ins = nc.tensor.transpose(xT_ps[n % 2][:, k * P:(k + 1) * P], xn_sb[:, i, k * P:(k + 1) * P], ident_sb[:])
                ins.then_inc(xnT_mm, 1)
                if after and i >= 1:
                    after(i - 1)
            if after:
                after(TT - 1)

        def moe_pe(pe, l):
            def logits(i):
                pe.wait_ge(xnT_copied, 2 * l * TT + i + 1)
                if i >= 6:
                    pe.wait_ge(index_ready, l * TT + i - 6 + 1)
                for k in range(KD):
                    ins = nc.tensor.matmul(logit_ps[i][:, 0:E], xnT[:, k, i * P:(i + 1) * P], gate_sb[:, k, :],
                                           start=(k == 0), stop=(k == KD - 1))
                ins.then_inc(logits_mm, 1)
            transpose_rows(pe, 2 * l, logits)
            pe.wait_ge(member_ready, l + 1)
            mem = member[:].rearrange("p t e -> p (t e)")
            nc.tensor.matmul(rank_ps[:, 0:TT * E], tri_sb[:, 0, :], mem, start=True, stop=True)
            nc.tensor.matmul(tot_ps[:, 0:TT * E], tri_sb[:, 1, :], mem, start=True, stop=True).then_inc(rank_mm, 1)
            for order_n, (k, i) in enumerate((k, i) for k in range(TOP_K) for i in range(TT)):
                n = i * TOP_K + k
                pe.wait_ge(hot_ready, l * PAIRS + order_n + 1)
                ins = nc.tensor.matmul(ids_ps[:, k * QW:(k + 1) * QW], hot_r[:, n, :], hot_q[:, n, :],
                                       start=(i == 0), stop=(i == TT - 1))
            ins.then_inc(ids_mm, 1)
            pe.wait_ge(tile_e_ready, l + 1)
            nc.tensor.transpose(tile_ps[0:1, 0:QW], tile_e[:, 0:1], ident_sb[0:QW, 0:QW]).then_inc(tile_e_mm, 1)

            pe.wait_ge(tiles_ready, l + 1)
            pe.wait_ge(ids_ready, l + 1)

            def rows_T(t):
                g, gn = slot_of(l, t, XG)
                s, n = slot_of(l, t)
                pe.wait_ge(xg_ready[l][t % XG], (t // XG + 1) * 16)
                pe.wait_ge(xgT_ready[s], n)
                for k in range(KD):
                    ins = nc.tensor.transpose(xT_ps[s][:, k * P:(k + 1) * P], xg[g][:, k * P:(k + 1) * P], ident_sb[:])
                ins.then_inc(xg_used[g], 1)

            def up(t, e, c):
                s, n = slot_of(l, t)
                pe.wait_ge(xgT_ready[s], n + 1)
                pe.wait_ge(act_ready[s], n)
                h2 = h_ps[s][:, 0:2 * WI].rearrange("p (a n) -> p a n", a=2)
                for k in range(KD):
                    w = w_exp_sb[:, bass.ds(e * EXP_COLS + k * 2 * MI, 2 * MI)]
                    nc.tensor.matmul(h2[:, :, 0:MI], xgT[s][:, k, :], w.rearrange("p (a n) -> p a n", a=2), start=(k == 0), stop=(k == KD - 1))
                for k in range(KD):
                    w = w_ch_sb[:, bass.ds(c * CH_COLS + k * 2 * CI, 2 * CI)]
                    ins = nc.tensor.matmul(h2[:, :, MI:WI], xgT[s][:, k, :], w.rearrange("p (a n) -> p a n", a=2), start=(k == 0), stop=(k == KD - 1))
                ins.then_inc(h_mm[s], 1)

            def act_T(t):
                s, n = slot_of(l, t)
                pe.wait_ge(act_ready[s], n + 1)
                pe.wait_ge(actT_ready[s], n)
                nc.tensor.transpose(aT_ps[s][0:MI, 0:P], act[s][:, 0:MI], ident_sb[:])
                nc.tensor.transpose(aT_ps[s][:, P:2 * P], act[s][:, MI:WI], ident_sb[:]).then_inc(actT_mm[s], 1)

            def down(t, e, c):
                s, n = slot_of(l, t)
                pe.wait_ge(actT_ready[s], n + 1)
                if l * SLOT_TILES + t >= 2:
                    pe.wait_ge(y_copied, l * SLOT_TILES + t - 1)
                nc.tensor.matmul(y_ps[s][:, 0:D], actT[s][0:MI, 0, :], w_down_sb[:, bass.ds(e * D, D)], start=True, stop=False)
                nc.tensor.matmul(y_ps[s][:, 0:D], actT[s][:, 1, :],
                                 w_ch_sb[:, bass.ds(c * CH_COLS + KD * 2 * CI, D)],
                                 start=False, stop=True).then_inc(y_mm[s], 1)

            held = {}

            def tiles(a, b):
                for t in range(a, b):
                    rows_T(t)
                    if t >= 3:
                        down(t - 3, *held[t - 3])
                    if l == 0 and t == 0:
                        pe.wait_ge(w_ready, NCH)
                    if t % LOAD == 0:
                        (_, es), (_, cs) = [nc.values_load_multi_w_load_instructions(
                            tile_ec[0:1, i, t:t + LOAD], engines=(mybir.EngineType.PE,), min_val=0, max_val=most,
                            skip_runtime_bounds_check_because="clamped to E - 1") for i, most in ((0, E - 1), (1, NCH - 1))]
                        for j in range(LOAD):
                            held[t + j] = es[j], cs[j]
                    up(t, *held[t])
                    if t >= 1:
                        act_T(t - 1)

            def drain(t):
                down(t - 3, *held[t - 3])
                act_T(t - 1)
                down(t - 2, *held[t - 2])
                down(t - 1, *held[t - 1])
                skip(pe, l, t, [xg_used, h_mm, actT_mm, y_mm])

            used = tiles_used(pe, l)
            tiles(0, MIN_TILES)
            grouped(pe, used, tiles, drain)

        def attention_pe(pe):
            def project(p):
                kind, n, b = p
                at = order.index(p)
                if at >= 1 and order[at - 1] in copied:
                    pe.wait_ge(v_copied, copied.index(order[at - 1]) + 1)
                elif at >= 1:
                    pe.wait_ge(rope_read, rotated.index(order[at - 1]) + 1)
                if kind == "q":
                    h = n // B
                    pe.wait_ge(wq_in[h % 2], (h // 2 + 1) * 16)
                    w = wq_sb[h % 2]
                else:
                    pe.wait_ge(kv_in, (n + 1) * 32)
                    w = wk_sb
                if kind == "v":
                    for t in range(SB):
                        for k in range(KD):
                            i = b * SB + t
                            ins = nc.tensor.matmul(proj_ps[:, t * DH:(t + 1) * DH], xnT[:, k, i * P:(i + 1) * P], wv_sb[:, k, :],
                                                   start=(k == 0), stop=(k == KD - 1))
                else:
                    for k in range(KD):
                        ins = nc.tensor.matmul(proj_ps[:, :], w[:, k, :], xnT[:, k, b * S:(b + 1) * S], start=(k == 0), stop=(k == KD - 1))
                ins.then_inc(proj_mm, 1)

            def scores(n, j):
                g, b = n // GU, n % B
                if j == 0:
                    pe.wait_ge(roped, rotated.index(("q", n, b)) + 1)
                pe.wait_ge(masked[j % 2], 2 * n + j // 2)
                nc.tensor.matmul(sc_ps[j % 2][:, 0:S - j * P], kT[g % 2][b][:, j * P:(j + 1) * P], qT[n % 2][:, j * P:],
                                 start=True, stop=True).then_inc(scores_mm, 1)

            def products(n):
                g, b = n // GU, n % B
                pe.wait_ge(o_copied, n)
                if n % GU == 0:
                    pe.wait_ge(v_copied, (g + 1) * B)
                for j in range(SB):
                    pe.wait_ge(masked[j % 2], 2 * n + j // 2 + 1)
                    ins = nc.tensor.matmul(o_ps[:, j * P:], v_sb[g % 2][:, b * SB + j, :], probs[j], start=(j == 0), stop=(j == SB - 1),
                                           skip_group_check=True)
                ins.then_inc(pv_mm, 1)

            def output(n):
                h = n // B
                pe.wait_ge(wo_in[h % 2], (h // 2 + 1) * 16)
                pe.wait_ge(o_copied, n + 1)
                for t in range(SB):
                    ins = nc.tensor.matmul(res_ps[(n % B) * SB + t], oT[n % 2][:, t * P:(t + 1) * P], wo_sb[h % 2], start=False, stop=False,
                                           skip_group_check=True)
                ins.then_inc(wo_mm, 1)

            pe.wait_ge(x_done, TT)
            for i in range(0, TT, 2):
                nc.tensor.matmul(bank[4 + i // 2][:, :], ident_sb[:], x_sb[:, i:i + 2, :], start=True, stop=False, skip_group_check=True)
            pe.wait_ge(xnT_copied, 2 * TT)
            for p in projections(-1, None):
                project(p)
            for n in range(UNITS):
                scores(n, 0)
                scores(n, 1)
                for p in projections(n, "scores"):
                    project(p)
                scores(n, 2)
                scores(n, 3)
                if n >= 1:
                    output(n - 1)
                for p in projections(n, "behind"):
                    project(p)
                products(n)
            output(UNITS - 1)

        @block.tensor
        def _(pe):
            pe.wait_ge(const_in, 16 * N_CONST)
            moe_pe(pe, 0)
            transpose_rows(pe, 1)
            attention_pe(pe)
            moe_pe(pe, 1)


def _constants():
    f = np.float32
    half = np.arange(0, DH, 2, dtype=f) / f(DH)
    inv_freq = (f(1.0) / np.power(f(10000.0), half)).astype(f)
    ang = np.arange(S, dtype=f)[:, None] * inv_freq[None, :]
    c, s = np.cos(ang).astype(f).T, np.sin(ang).astype(f).T
    cos = np.concatenate([c, c], 0)
    sin = np.concatenate([s, -s], 0)
    lam = np.exp2(-8.0 * np.arange(1, H + 1, dtype=f) / f(H)).astype(f)
    diff = np.arange(S, dtype=f)[None, :] - np.arange(P, dtype=f)[:, None]
    decay = np.where(diff[None] >= 0, np.exp(-lam[:, None, None] * np.maximum(diff, 0)[None]), 0.0).astype(f)
    ident = np.eye(P, dtype=f)
    tri = np.stack([np.triu(np.ones((P, P)), 1), np.ones((P, P))], 1).astype(np.float16)
    p = np.arange(P)[:, None]
    row = lambda a: np.tile(a, (P, 1))
    iotas = np.concatenate([row(np.arange(E)), row(P * np.arange(TT)), p + P * np.arange(TT)[None, :] + 1, row(np.arange(TOP_K)),
                            p, TOP_K * T + p + P * np.arange(QW)[None, :] + TOP_K], 1).astype(f)
    iota16 = row(np.arange(P)).astype(np.float16)
    keep = np.tile(np.tile(np.r_[0.0, np.ones(TT - 1)], E), (P, 1)).astype(f)
    return dict(decay=decay, cos=cos, sin=sin, ident=ident, tri=tri, iotas=iotas, iota16=iota16, scan_keep=keep)


def kernel(L0_attn_x, L0_attn_wq, L0_attn_wk, L0_attn_wv, L0_attn_wo, L0_ffn_gate_w, L0_ffn_Wg, L0_ffn_Wu, L0_ffn_Wd,
           L0_ffn_cWg, L0_ffn_cWu, L0_ffn_cWd):
    import concourse.bacc as _bacc
    from concourse import mybir as _mybir
    from concourse.bass_utils import run_bass_kernel_spmd as _run

    def contract_first(w, heads):
        w = np.asarray(w)
        return w.reshape(heads, -1, KD, P).transpose(0, 3, 2, 1).reshape(heads, P, -1)

    wg, wu, wd = np.asarray(L0_ffn_Wg), np.asarray(L0_ffn_Wu), np.asarray(L0_ffn_Wd)
    cg, cu, cd = np.asarray(L0_ffn_cWg), np.asarray(L0_ffn_cWu), np.asarray(L0_ffn_cWd)
    up = np.stack([wg, wu], 2).reshape(NCH, 2, KD, P, 2 * MI).transpose(0, 3, 1, 2, 4).reshape(NCH, P, -1)
    cup = np.stack([cg, cu], 2).reshape(NCH, KD, P, 2 * CI).transpose(0, 2, 1, 3).reshape(NCH, P, -1)
    arrays = dict(
        x_in=np.asarray(L0_attn_x).reshape(T, D),
        gate=np.asarray(L0_ffn_gate_w).reshape(E, KD, P).transpose(2, 1, 0),
        w_exp=up, w_ch=np.concatenate([cup, cd], 2),
        w_down=wd.reshape(NCH, 2, MI, D).transpose(0, 2, 1, 3).reshape(NCH, MI, 2 * D),
        wq=contract_first(L0_attn_wq, H), wk=contract_first(L0_attn_wk, HKV), wv=contract_first(L0_attn_wv, HKV),
        wo=np.asarray(L0_attn_wo).reshape(D, H, DH).transpose(1, 2, 0),
        **_constants())
    nc = _bacc.Bacc("TRN2", target_bir_lowering=False, num_devices=1)
    args = {}
    for name, a in arrays.items():
        arrays[name] = a = np.ascontiguousarray(a)
        args[name] = nc.dram_tensor(name, a.shape, _mybir.dt.from_np(a.dtype), kind="ExternalInput").ap()
    args["out"] = nc.dram_tensor("out", (T, D), _mybir.dt.float32, kind="ExternalOutput").ap()
    macaron_kernel(nc, **args)
    r = _run(nc, [arrays], core_ids=[0])
    return r.results[0]["out"].reshape(B, S, D)
```

```python
import numpy as np
import concourse.bass as bass
from concourse import mybir
from contextlib import ExitStack

P = 128
B, S, D = 2, 512, 256
T = B * S
TT = T // P
SB = S // P
KD = D // P
H, HKV, DH = 16, 4, 128
GROUPS = H // HKV
E, TOP_K, MI = 32, 4, 96
NCH, CI = 16, 128
SMALL_SCALE = 0.05
EPS = 1e-5
PAIRS = TT * TOP_K
SLOT_TILES = PAIRS + E - 1
MIN_TILES = T * TOP_K // P
GROUP = 2
QW = SLOT_TILES + 1
LOAD = 4
XG, YB, ZB = 4, 4, 6
LAG = 8
HALF = S // 2
DEPTH = 2
BEHIND = 7
WI = MI + CI
EXP_COLS = KD * 2 * MI
CH_COLS = KD * 2 * CI + D


def macaron_kernel(nc, x_in, gate, w_exp, w_ch, w_down, wq, wk, wv, wo, decay, key_decay, cos, sin, ident, tri, iotas, iota16, scan_keep, out):
    f32, f16, i32, u32 = mybir.dt.float32, mybir.dt.float16, mybir.dt.int32, mybir.dt.uint32
    f32r = mybir.dt.float32r
    ALU = mybir.AluOpType
    ACT = mybir.ActivationFunctionType
    AX = mybir.AxisListType

    ctx = ExitStack()
    with ctx:
        def sb(name, shape, dt=f32):
            return ctx.enter_context(nc.sbuf_tensor(name, shape, dt))

        def sem(name):
            return ctx.enter_context(nc.semaphore(name))

        def sems(name, n):
            return [sem(f"{name}{i}") for i in range(n)]

        xn_dram = [nc.dram_tensor(f"xn_dram{l}", (T, D), f32).ap() for l in range(2)]
        z_dram = [nc.dram_tensor(f"z_dram{l}", (T * TOP_K + SLOT_TILES * P, D), f32).ap() for l in range(2)]

        w_ch_sb = sb("w_ch_sb", [P, NCH * CH_COLS])
        w_down_sb = sb("w_down_sb", [MI, E * D])
        gate_sb = sb("gate_sb", [P, KD, E])
        x_sb = sb("x_sb", [P, TT, D])
        xn_sb = sb("xn_sb", [P, TT, D])
        xnT = sb("xnT", [P, KD, T])
        ident_sb = sb("ident_sb", [P, P])
        tri_sb = sb("tri_sb", [P, 2, P], f16)
        iotas_sb = sb("iotas_sb", [P, E + TT + TT + TOP_K + 1 + QW])
        iota_e = iotas_sb[:, 0:E]
        thr_sb = iotas_sb[:, E:E + TT]
        tok1 = iotas_sb[:, E + TT:E + 2 * TT]
        iota_k = iotas_sb[:, E + 2 * TT:E + 2 * TT + TOP_K]
        part = iotas_sb[:, E + 2 * TT + TOP_K:][:, 0:1]
        dump = iotas_sb[:, E + 2 * TT + TOP_K + 1:]
        iota16_sb = sb("iota16_sb", [P, P], f16)
        scan_keep_sb = sb("scan_keep_sb", [P, E * TT])
        stats = sb("stats", [P, 2, 6])
        mv = sb("mv", [P, TT, 2])
        var_eps = sb("var_eps", [P, TT])
        rvar = sb("rvar", [P, TT])
        rstd = sb("rstd", [P, TT])

        table_warm = sb("table_warm", [P, 3])

        top = sb("top", [P, TT, 8])
        top_ix = sb("top_ix", [P, TT, 8], u32)
        ixf = sb("ixf", [P, TT, TOP_K])
        member2 = sb("member2", [P, 2, TT, E], f16)
        member = sb("member", [P, TT, E], f16)
        top_rel = sb("top_rel", [P, TT, TOP_K])
        top_exp = sb("top_exp", [P, TT, TOP_K])
        top_sum = sb("top_sum", [P, TT])
        wgt = sb("wgt", [P, TT, TOP_K])
        ntile = sb("ntile", [P, E])
        ntile_incl = sb("ntile_incl", [P, E])
        ntile_excl = sb("ntile_excl", [P, E])
        ones_e = sb("ones_e", [P, E])
        slot_base = sb("slot_base", [P, E, TT])
        slot_te = sb("slot_te", [P, TT, E])
        slotf = sb("slotf", [P, TT * TOP_K])
        slot_ix = sb("slot_ix", [P, TT * TOP_K], i32)
        slot_qi = sb("slot_qi", [P, TT * TOP_K], i32)
        slot_ri = sb("slot_ri", [P, TT * TOP_K], i32)
        slot_q = sb("slot_q", [P, TT * TOP_K])
        slot_r = sb("slot_r", [P, TT * TOP_K])
        n_used = sb("n_used", [1, 1], i32)
        tile_ge = sb("tile_ge", [QW, E])
        tile_e = sb("tile_e", [QW, 1])
        tile_ec = sb("tile_ec", [1, 2, QW], i32)
        ids = sb("ids", [P, QW], i32)
        ids_sum = sb("ids_sum", [P, QW])
        dest_k = sb("dest_k", [P, QW])
        dest_empty = sb("dest_empty", [P, QW])
        dest = sb("dest", [P, QW], i32)


        rot = sb("rot", [P, 2, S])
        cos_sb, sin_sb = rot[:, 0, :], rot[:, 1, :]
        wkv_sb = sb("wkv_sb", [P, 2, KD, DH])
        wk_sb, wv_sb = wkv_sb[:, 0, :, :], wkv_sb[:, 1, :, :]
        wq_all = sb("wq_all", [P, 2, KD, DH])
        wq_sb = [wq_all[:, u, :, :] for u in range(2)]
        wo_all = sb("wo_all", [P, 2, D])
        wo_sb = [wo_all[:, u, :] for u in range(2)]
        decay_all = sb("decay_all", [P, 2, S])
        decay_sb = [decay_all[:, u, :] for u in range(2)]
        rope = sb("rope", [P, 4, S])
        rope_a, rope_b = [rope[:, u, :] for u in range(2)], [rope[:, 2 + u, :] for u in range(2)]
        kqT = sb("kqT", [P, 4, S])
        v_all = sb("v_all", [P, TT * DH])
        xn_flat = xn_sb[:, :, :].rearrange("p t d -> p (t d)")
        kT = [[kqT[:, b, :] for b in range(B)], [xn_flat[:, b * S:(b + 1) * S] for b in range(B)]]
        qT = [kqT[:, 2 + u, :] for u in range(2)]
        v_sb = [v_all[:, :].rearrange("p (t d) -> p t d", t=TT),
                xn_flat[:, B * S:2 * B * S].rearrange("p (t d) -> p t d", t=TT)]
        probs_all = sb("probs_all", [P, TOP_K * D])
        PAIR = HALF + P
        probs = [probs_all[:, c * PAIR:(c + 1) * PAIR] for c in range(2)]
        key_decay_sb = sb("key_decay_sb", [P, 2 * H])
        oT_all = sb("oT_all", [P, 2 * S])
        oT = [oT_all[:, u * S:(u + 1) * S] for u in range(2)]
        with nc.sbuf_tensor("w_exp_sb", [P, E * EXP_COLS], f32) as w_exp_sb:
            pass
        split_sb = sb("split_sb", [P, 2 * KD * T + 4 * S + 10 * D], f32r)
        state_sb = sb("state_sb", [P, E * EXP_COLS - (2 * KD * T + 4 * S + 10 * D)])
        k_tok = [[state_sb[:, (2 * a + b) * HALF:(2 * a + b + 1) * HALF].rearrange("p (t d) -> p t d", d=DH) for b in range(B)]
                 for a in range(2)]
        v_dec, q_dec = [[state_sb[:, (4 + 2 * a + u) * HALF:(5 + 2 * a + u) * HALF] for u in range(2)] for a in range(2)]
        state = [state_sb[:, 8 * HALF + u * DH:8 * HALF + (u + 1) * DH] for u in range(2)]
        room = split_sb[:, :]
        xnT_hi = room[:, 0:KD * T].rearrange("p (k t) -> p k t", k=KD)
        xnT_lo = room[:, KD * T:2 * KD * T].rearrange("p (k t) -> p k t", k=KD)
        room = room[:, 2 * KD * T:]
        oT_hi, oT_lo = [[room[:, (2 * a + u) * S:(2 * a + u + 1) * S] for u in range(2)] for a in range(2)]
        room = room[:, 4 * S:]
        w_whole = {("q", u): wq_all[:, u, :, :].rearrange("p k n -> p (k n)") for u in range(2)}
        w_whole |= {("o", u): wo_sb[u] for u in range(2)}
        w_whole |= {("k", 0): wkv_sb[:, 0, :, :].rearrange("p k n -> p (k n)")}
        w_hi, w_lo = [{key: room[:, (a + 5 * b) * D:(a + 5 * b + 1) * D] for a, key in enumerate(w_whole)} for b in range(2)]
        chosen = probs_all[:, 0:TT * TOP_K * E].rearrange("p (t k e) -> p t k e", t=TT, k=TOP_K)
        over = wo_all[:, 0, :].rearrange("p (e t) -> p e t", t=TT)
        tot_incl, tot_excl = [wq_all[:, a, :, :].rearrange("p k n -> p (k n)").rearrange("p (e t) -> p e t", t=TT)
                              for a in range(2)]
        xg = [decay_all[:, u // 2, (u % 2) * D:(u % 2 + 1) * D] for u in range(XG)]
        xgT = [oT_all[:, u * D:(u + 1) * D].rearrange("p (k t) -> p k t", k=KD) for u in range(2)]
        silu_g = [rot[:, 0, u * WI:(u + 1) * WI] for u in range(2)]
        act = [rot[:, 1, u * WI:(u + 1) * WI] for u in range(2)]
        actT = [wkv_sb[:, u, :, :] for u in range(2)]
        y_sb = [probs_all[:, u * D:(u + 1) * D] for u in range(YB)]
        z_rooms = [kqT[:, 0:2, :].rearrange("p a s -> p (a s)"), kqT[:, 2:4, :].rearrange("p a s -> p (a s)"),
                   rope[:, 0:2, :].rearrange("p a s -> p (a s)"), rope[:, 2:4, :].rearrange("p a s -> p (a s)"),
                   oT_all[:, :], probs_all[:, 0:TOP_K * D]]
        z_sb = [room.rearrange("p (k d) -> p k d", d=D) for room in z_rooms]
        hot_r = rope[:, :, :].rearrange("p a s -> p (a s)").bitcast(f16).rearrange("p (n r) -> p n r", r=P)
        hot_q = v_all[:, :].bitcast(f16).rearrange("p (n q) -> p n q", q=QW)
        slot_pick = oT_all[:, :].rearrange("p (t k e) -> p t k e", t=TT, k=TOP_K)
        dest_hot = kqT[:, 0, 0:TOP_K * QW].rearrange("p (k q) -> p k q", q=QW)

        bank = [ctx.enter_context(nc.psum_tensor(f"bank{i}", [P, 512], f32)) for i in range(8)]
        xT_ps = [bank[0], bank[1]]
        logit_ps = [bank[2 + i % 6] for i in range(TT)]
        rank_ps, tot_ps, ids_ps, tile_ps = bank[3], bank[4], bank[5], bank[6]
        h_ps, aT_ps, y_ps = [bank[2], bank[3]], [bank[4], bank[5]], [bank[6], bank[7]]
        o_ps, sc_ps = bank[1], [bank[2], bank[3]]
        res_ps = [bank[4 + i // 2][:, (i % 2) * D:(i % 2 + 1) * D] for i in range(TT)]

        gate_in, const_in = sem("gate_in"), sem("const_in")
        x_loaded = sems("x_loaded", TT)
        w_in = sems("w_in", NCH)
        dve_step = sem("dve_step")
        rvar_ready, rstd_ready = sem("rvar_ready"), sem("rstd_ready")
        xn_ready, xnT_mm, xnT_copied = sem("xn_ready"), sem("xnT_mm"), sem("xnT_copied")
        xn_stored = sems("xn_stored", 2)
        logits_mm = sem("logits_mm")
        top_ready, index_ready, rel_ready, exp_ready = sem("top_ready"), sem("index_ready"), sem("rel_ready"), sem("exp_ready")
        member_ready, rank_mm = sem("member_ready"), sem("rank_mm")
        used_ready = sem("used_ready")
        slot_r_ready, hot_r_by_pool, hot_q_ready = sem("slot_r_ready"), sem("hot_r_by_pool"), sem("hot_q_ready")
        hot_r_by_dve, tile_e_ready, tile_e_mm = sem("hot_r_by_dve"), sem("tile_e_ready"), sem("tile_e_mm")
        ids_mm, ids_ready, tiles_ready, dest_ready = sem("ids_mm"), sem("ids_ready"), sem("tiles_ready"), sem("dest_ready")
        w_split_hi, w_split, xnT_split, o_split = sem("w_split_hi"), sem("w_split"), sem("xnT_split"), sem("o_split")
        w_reloaded = sem("w_reloaded")
        w_ready = sem("w_ready")
        xg_used = sems("xg_used", XG)
        xg_ready = [sems(f"xg_ready{l}_", XG) for l in range(2)]
        y_scattered = [sems(f"y_scattered{l}_", YB) for l in range(2)]
        results_stored = sem("results_stored")
        xgT_ready = sems("xgT_ready", 2)
        h_mm, silu_ready, act_ready = sems("h_mm", 2), sems("silu_ready", 2), sems("act_ready", 2)
        actT_mm, actT_ready = sems("actT_mm", 2), sems("actT_ready", 2)
        y_mm, y_copied = sems("y_mm", 2), sem("y_copied")
        z_in, z_scaled, x_part = sems("z_in", ZB), sem("z_scaled"), sem("x_part")
        x_done = sem("x_done")
        out_stored = sem("out_stored")
        kv_in, wq_in, wo_in, decay_in = sem("kv_in"), sems("wq_in", 2), sems("wo_in", 2), sems("decay_in", 2)
        kv_copied = sem("kv_copied")
        proj_mm, rope_read, roped = sem("proj_mm"), sem("rope_read"), sem("roped")
        scores_mm, masked = sem("scores_mm"), sems("masked", 2)
        v_scaled, q_scaled = sem("v_scaled"), sem("q_scaled")
        pv_mm, o_copied, wo_mm = sem("pv_mm"), sem("o_copied"), sem("wo_mm")
        x2_copied = sem("x2_copied")

        N_CONST = 5

        def slot_of(l, t, buffers=2):
            n = l * SLOT_TILES + t
            return n % buffers, n // buffers

        def uses(l, t, s, buffers):
            return (l * SLOT_TILES + t - s + buffers - 1) // buffers

        def skip(eng, l, t, rings):
            for ring in rings:
                for s, signal in enumerate(ring):
                    eng.wait_ge(signal, uses(l, t, s, len(ring)))
                    left = uses(l + 1, 0, s, len(ring)) - uses(l, t, s, len(ring))
                    if left:
                        eng.sem_inc(signal, left)

        def tiles_used(eng, l):
            eng.wait_ge(used_ready, l + 1)
            return eng.value_load(n_used[0:1, 0:1], min_val=MIN_TILES, max_val=SLOT_TILES)

        def grouped(eng, used, tiles, drain, t=MIN_TILES):
            if t >= SLOT_TILES:
                drain(SLOT_TILES)
                return
            end = min(t + GROUP, SLOT_TILES)
            with eng.If(used > t):
                tiles(t, end)
                grouped(eng, used, tiles, drain, end)
            with eng.Else():
                drain(t)

        UNITS, GU = H * B, GROUPS * B

        def projections(n, place):
            g, m = n // GU, n % GU
            if n < 0:
                return [("q", 0, 0), ("k", 0, 0), ("v", 0, 0), ("v", 0, 1), ("k", 0, 1), ("t", 0, 0)]
            if place == "scores":
                return [("q", n + 1, (n + 1) % B)] if n + 1 < UNITS else []
            if g + 1 < HKV and m >= 2:
                return [("vvkktt"[m - 2], g + 1, m % 2)]
            return [("t", 0, 1)] if n == 0 else []

        def splits(n):
            if n < 0:
                return [("q", 0), ("k", 0)]
            found = [("o", n // 2)] if n % 2 == 0 else [("q", (n + 3) // 2)] if n + 3 < UNITS else []
            if n == 0:
                found.append(("q", 1))
            if n % GU == 3 and n // GU + 1 < HKV:
                found.append(("k", n // GU + 1))
            return found

        def split_buffer(key):
            kind, n = key
            return (kind, 0 if kind == "k" else n % 2)

        pairs = [i * TOP_K + k for k in range(TOP_K) for i in range(TT)]
        pool_hot = [n for at, n in enumerate(pairs) if at % 16 in (1, 3, 4, 6, 9, 11, 14)]

        split_order = [key for n in range(-1, UNITS) for key in splits(n)]
        order = projections(-1, None)
        for n in range(UNITS):
            order += projections(n, "scores") + projections(n, "behind")
        rotated = [p for p in order if p[0] in "qk"]
        copied = [p for p in order if p[0] in "vt"]
        proj_bank = [bank[a] for a in (2, 3, 6, 0, 1)] + [bank[0]] * (len(order) - 5)

        block = ctx.enter_context(nc.Block())

        def load_results(sp, l, between=None):
            sp.wait_ge(results_stored, l + 1)
            for i in range(TT):
                n = l * TT + i
                if between and i == ZB:
                    between()
                if n >= ZB:
                    sp.wait_ge(x_done, n - ZB + 1)
                sp.dma_start(z_sb[n % ZB], z_dram[l][i * P * TOP_K:(i + 1) * P * TOP_K, :]
                             .rearrange("(p k) d -> p k d", k=TOP_K)).then_inc(z_in[n % ZB], 16)

        @block.sync
        def _(sp):
            for i in range(TT):
                sp.dma_start(x_sb[:, i, :], x_in[i * P:(i + 1) * P, :]).then_inc(x_loaded[i], 16)
                if i == 1:
                    sp.dma_start(ident_sb[:], ident[:, :]).then_inc(gate_in, 16)
                    sp.dma_start(gate_sb[:], gate[:, :, :]).then_inc(gate_in, 16)
            sp.dma_start(tri_sb[:], tri[:, :, :]).then_inc(const_in, 16)
            sp.dma_start(iota16_sb[:], iota16[:, :]).then_inc(const_in, 16)
            sp.dma_start(iotas_sb[:], iotas[:, :]).then_inc(const_in, 16)
            sp.dma_start(scan_keep_sb[:], scan_keep[:, :]).then_inc(const_in, 16)
            sp.dma_start(key_decay_sb[:], key_decay[:, :]).then_inc(const_in, 16)

            def load_chunk(c):
                sp.dma_start(w_exp_sb[:, 2 * c * EXP_COLS:2 * (c + 1) * EXP_COLS], w_exp[c, :, :]).then_inc(w_in[c], 16)
                sp.dma_start(w_ch_sb[:, c * CH_COLS:(c + 1) * CH_COLS], w_ch[c, :, :]).then_inc(w_in[c], 16)
                sp.dma_start(w_down_sb[:, c * 2 * D:(c + 1) * 2 * D], w_down[c, :, :]).then_inc(w_in[c], 16)

            def count_chunk(c):
                sp.wait_ge(w_in[c], 48)
                sp.sem_inc(w_ready, 1)

            for c in range(NCH - BEHIND):
                load_chunk(c)
            for c in range(NCH - BEHIND - DEPTH):
                count_chunk(c)
            for c in range(NCH - BEHIND, NCH):
                sp.wait_ge(xg_ready[0][max(0, c - (NCH - XG))], 16)
                count_chunk(c - DEPTH)
                load_chunk(c)
            for c in range(NCH - DEPTH, NCH):
                count_chunk(c)

            def load_kv(g):
                if g >= 1:
                    sp.wait_ge(proj_mm, max(order.index((kind, g - 1, 1)) for kind in "kv") + 1)
                sp.dma_start(wk_sb, wk[g, :, :]).then_inc(kv_in, 16)
                sp.dma_start(wv_sb, wv[g, :, :]).then_inc(kv_in, 16)

            def load_head(h):
                u = h % 2
                if h >= 2:
                    sp.wait_ge(proj_mm, order.index(("q", 2 * (h - 2) + 1, 1)) + 1)
                sp.dma_start(wq_sb[u], wq[h, :, :]).then_inc(wq_in[u], 16)
                if h >= 2:
                    sp.wait_ge(pv_mm, B * (h - 1))
                sp.dma_start(decay_sb[u], decay[h, :, :]).then_inc(decay_in[u], 16)
                if h >= 2:
                    sp.wait_ge(wo_mm, 2 * (h - 1))
                sp.dma_start(wo_sb[u], wo[h, :, :]).then_inc(wo_in[u], 16)

            def first_loads():
                load_kv(0)
                load_head(0)
                sp.dma_start(cos_sb, cos[:, :]).then_inc(const_in, 16)
                sp.dma_start(sin_sb, sin[:, :]).then_inc(const_in, 16)

            load_results(sp, 0, first_loads)
            for h in range(1, H):
                load_head(h)
                if h % GROUPS == 1 and h // GROUPS + 1 < HKV:
                    load_kv(h // GROUPS + 1)

            sp.wait_ge(wo_mm, UNITS)
            for c in range(NCH):
                sp.dma_start(w_exp_sb[:, 2 * c * EXP_COLS:2 * (c + 1) * EXP_COLS], w_exp[c, :, :]).then_inc(w_reloaded, 16)
            load_results(sp, 1)
            for i in range(TT):
                sp.wait_ge(x_done, TT + i + 1)
                sp.dma_start(out[i * P:(i + 1) * P, :], x_sb[:, i, :]).then_inc(out_stored, 16)
            sp.wait_ge(out_stored, 16 * TT)

        def split_lo(pool, key):
            buffer = split_buffer(key)
            pool.wait_ge(w_split_hi, split_order.index(key) + 1)
            nc.gpsimd.tensor_tensor(w_lo[buffer], w_whole[buffer], w_hi[buffer].bitcast(f32),
                                    ALU.subtract).then_inc(w_split, 1)

        def one_hot_r(eng, n):
            return eng.tensor_scalar(hot_r[:, n, :], iota16_sb[:], slot_r[:, n:n + 1], None, ALU.is_equal)

        def moe_pool(pool, l):
            pool.wait_ge(slot_r_ready, l + 1)
            for n in pool_hot:
                one_hot_r(nc.gpsimd, n).then_inc(hot_r_by_pool, 1)
            pool.wait_ge(xn_stored[l], 16 * TT)
            pool.wait_ge(ids_ready, l + 1)

            def gather(t):
                s, n = slot_of(l, t, XG)
                pool.wait_ge(xg_used[s], n)
                pool.indirect_dma_start(out=xg[s], out_offset=None, in_=xn_dram[l][:, :],
                                        in_offset=bass.IndirectOffsetOnAxis(ap=ids[:, t:t + 1], axis=0)
                                        ).then_inc(xg_ready[l][t % XG], 16)

            def scatter(t):
                s, n = slot_of(l, t, YB)
                if t == 0:
                    pool.wait_ge(dest_ready, l + 1)
                pool.wait_ge(y_copied, l * SLOT_TILES + t + 1)
                pool.indirect_dma_start(out=z_dram[l][:, :],
                                        out_offset=bass.IndirectOffsetOnAxis(ap=dest[:, t:t + 1], axis=0),
                                        in_=y_sb[s], in_offset=None).then_inc(y_scattered[l][t % YB], 16)

            def tiles(a, b):
                for t in range(a, b):
                    gather(t)
                    if t >= LAG:
                        scatter(t - LAG)

            def drain(t):
                for u in range(t - LAG, t):
                    scatter(u)
                for u in range(YB):
                    pool.wait_ge(y_scattered[l][u], 16 * uses(0, t, u, YB))
                pool.sem_inc(results_stored, 1)

            tiles(0, MIN_TILES)
            grouped(pool, tiles_used(pool, l), tiles, drain)

            lag = 0 if l else 5
            for i in range(TT + lag):
                n = l * TT + i
                if i < TT:
                    pool.wait_ge(z_scaled, n + 1)
                    nc.gpsimd.tensor_tensor(x_sb[:, i, :], x_sb[:, i, :], z_sb[n % ZB][:, TOP_K - 1, :], ALU.add).then_inc(x_part, 1)
                if l == 0 and i == TT - 1:
                    for key in splits(-1):
                        split_lo(pool, key)
                if l == 0 and i >= lag:
                    pool.wait_ge(xnT_copied, TT + i - lag + 1)
                    cols = slice((i - lag) * P, (i - lag + 1) * P)
                    nc.gpsimd.tensor_tensor(xnT_lo[:, :, cols], xnT[:, :, cols], xnT_hi[:, :, cols].bitcast(f32),
                                            ALU.subtract).then_inc(xnT_split, 1)

        @block.gpsimd
        def _(pool):
            moe_pool(pool, 0)
            def add_rotated(p):
                r = rotated.index(p)
                kind, n, b = p
                pool.wait_ge(rope_read, r + 1)
                if kind == "k":
                    if n >= 2:
                        pool.wait_ge(scores_mm, (n - 1) * GU * 2)
                    dst = kT[n % 2][b]
                else:
                    if n >= 2:
                        pool.wait_ge(scores_mm, (n - 1) * 2)
                    dst = qT[n % 2]
                nc.gpsimd.tensor_tensor(dst, rope_a[r % 2], rope_b[r % 2], ALU.add).then_inc(roped, 1)
                if kind == "q":
                    h = n // B
                    pool.wait_ge(roped, r + 1)
                    pool.wait_ge(decay_in[h % 2], (h // 2 + 1) * 16)
                    if n >= 2:
                        pool.wait_ge(pv_mm, n - 1)
                    nc.gpsimd.tensor_tensor(q_dec[n % 2], dst[:, HALF:], decay_sb[h % 2][:, HALF:], ALU.mult).then_inc(q_scaled, 1)

            for n in range(-1, UNITS):
                for p in projections(n, "scores"):
                    if p in rotated:
                        add_rotated(p)
                if n >= 0:
                    for key in splits(n):
                        split_lo(pool, key)
                    for p in projections(n, "behind"):
                        if p in rotated:
                            add_rotated(p)
            moe_pool(pool, 1)

        def split_hi(act_e, key):
            kind, n = key
            if kind == "k":
                act_e.wait_ge(kv_in, (n + 1) * 32)
            else:
                act_e.wait_ge({"q": wq_in, "o": wo_in}[kind][n % 2], (n // 2 + 1) * 16)
            buffer = split_buffer(key)
            nc.scalar.activation(w_hi[buffer], w_whole[buffer], ACT.Copy).then_inc(w_split_hi, 1)

        def copy_projected(act_e, p):
            kind, g, b = p
            act_e.wait_ge(proj_mm, order.index(p) + 1)
            src = proj_bank[order.index(p)]
            if kind == "v":
                if g >= 2:
                    act_e.wait_ge(pv_mm, (g - 1) * GU)
                dst, src = v_sb[g % 2][:, b * SB:(b + 1) * SB, :], src[:, :]
            else:
                if g >= 2:
                    act_e.wait_ge(scores_mm, (g - 1) * GU * 2)
                dst, src = k_tok[g % 2][b], src[:, 0:HALF]
            nc.scalar.activation(dst, src.rearrange("p (t d) -> p t d", d=DH), ACT.Copy).then_inc(kv_copied, 1)

        def scale_values(act_e, n):
            g, h, b = n // GU, n // B, n % B
            act_e.wait_ge(kv_copied, copied.index(("v", g, b)) + 1)
            if n >= 2:
                act_e.wait_ge(scores_mm, 2 * (n - 2) + 1)
            for t in range(2):
                ins = nc.scalar.activation(v_dec[n % 2][:, t * DH:(t + 1) * DH], v_sb[g % 2][:, b * SB + t, :], ACT.Copy,
                                           scale=key_decay_sb[:, 2 * h + t:2 * h + t + 1])
            ins.then_inc(v_scaled, 1)

        def scale_results(act_e, l, i):
            n = l * TT + i
            act_e.wait_ge(z_in[n % ZB], 16 * (n // ZB + 1))
            z = z_sb[n % ZB][:, TOP_K - 1, :]
            nc.scalar.activation(z, z, ACT.Copy, scale=wgt[:, i, TOP_K - 1:TOP_K]).then_inc(z_scaled, 1)

        def norm_act(act_e, s, beside=None):
            def transposed(i):
                n = s * TT + i
                if s != 1:
                    act_e.wait_ge(xn_ready, n + 1)
                    act_e.dma_start(xn_dram[s // 2][i * P:(i + 1) * P, :], xn_sb[:, i, :]).then_inc(xn_stored[s // 2], 16)
                act_e.wait_ge(xnT_mm, n + 1)
                rows = xT_ps[n % 2][:, 0:D].rearrange("p (k t) -> p k t", k=KD)
                ins = nc.scalar.activation(xnT[:, :, i * P:(i + 1) * P], rows, ACT.Copy)
                if s == 1:
                    ins = nc.scalar.activation(xnT_hi[:, :, i * P:(i + 1) * P], rows, ACT.Copy)
                ins.then_inc(xnT_copied, 1)
            if s >= 1:
                nc.scalar.activation(table_warm[:, s:s + 1], ones_e[:, s:s + 1], ACT.Sqrt)
            if s == 1:
                for i in range(3):
                    scale_results(act_e, 0, i)
            for i in range(TT):
                n = s * TT + i
                if s == 1 and i + 3 < TT:
                    scale_results(act_e, 0, i + 3)
                act_e.wait_ge(rvar_ready, n + 1)
                nc.scalar.activation(rstd[:, i:i + 1], rvar[:, i:i + 1], ACT.Sqrt).then_inc(rstd_ready, 1)
                if i == 2 and beside:
                    beside()
                lag = 2 if s >= 1 else 1
                if i >= lag:
                    transposed(i - lag)
                if s == 1 and i == TT - 3:
                    for key in splits(-1):
                        split_hi(act_e, key)
            for i in range(TT - lag, TT):
                transposed(i)

        def moe_act(act_e, l, beside=None):
            norm_act(act_e, 2 * l, beside)
            act_e.wait_ge(rel_ready, l + 1)
            nc.scalar.activation(top_exp[:], top_rel[:], ACT.Exp).then_inc(exp_ready, 1)

            used = tiles_used(act_e, l)

            def silu(t):
                s, n = slot_of(l, t)
                act_e.wait_ge(h_mm[s], n + 1)
                act_e.wait_ge(act_ready[s], n)
                nc.scalar.activation(silu_g[s], h_ps[s][:, 0:WI], ACT.Silu).then_inc(silu_ready[s], 1)

            def results_out(t):
                s, n = slot_of(l, t)
                act_e.wait_ge(y_mm[s], n + 1)
                y, _ = slot_of(l, t, YB)
                if t >= YB:
                    act_e.wait_ge(y_scattered[l][t % YB], t // YB * 16)
                nc.scalar.activation(y_sb[y], y_ps[s][:, 0:D], ACT.Copy).then_inc(y_copied, 1)

            def tiles(a, b):
                for t in range(a, b):
                    silu(t)
                    if t >= 2:
                        results_out(t - 2)

            def drain(t):
                results_out(t - 2)
                results_out(t - 1)
                skip(act_e, l, t, [silu_ready, [y_copied]])

            tiles(0, MIN_TILES)
            grouped(act_e, used, tiles, drain)

        @block.scalar
        def _(act_e):
            moe_act(act_e, 0)
            norm_act(act_e, 1)
            copy_projected(act_e, ("v", 0, 0))
            scale_values(act_e, 0)
            copy_projected(act_e, ("v", 0, 1))
            copy_projected(act_e, ("t", 0, 0))

            def residual_out(i):
                act_e.wait_ge(wo_mm, UNITS - 1 if i < SB else UNITS)
                nc.scalar.activation(x_sb[:, i, :], res_ps[i], ACT.Copy).then_inc(x2_copied, 1)

            for n in range(UNITS):
                if n + 1 < UNITS:
                    scale_values(act_e, n + 1)
                for key in splits(n):
                    split_hi(act_e, key)
                for p in projections(n, "behind"):
                    if p in copied:
                        copy_projected(act_e, p)
                if n == UNITS - 1:
                    for i in range(SB):
                        residual_out(i)
                act_e.wait_ge(pv_mm, n + 1)
                if n >= 2:
                    act_e.wait_ge(wo_mm, n - 1)
                nc.scalar.activation(oT_hi[n % 2], o_ps[:, :], ACT.Copy).then_inc(o_copied, 1)
            def last_residuals():
                for i in range(SB, TT):
                    residual_out(i)

            moe_act(act_e, 1, last_residuals)
            for i in range(TT):
                scale_results(act_e, 1, i)

        def norm_dve(dve, tick, s, beside=None):
            done = {}

            def after(key):
                if key in done:
                    dve.wait_ge(dve_step, done[key])

            def add(i, k):
                if s == 1 and 0 <= i < TT:
                    after(("add", i, k - 1))
                    ins = combine(dve, 0, i, k)
                    if k < TOP_K - 2:
                        done["add", i, k] = tick(ins)
                    else:
                        ins.then_inc(x_done, 1)

            def stats_of(i):
                if 0 <= i < TT:
                    if s == 0:
                        dve.wait_ge(x_loaded[i], 16)
                    if s == 2:
                        dve.wait_ge(x2_copied, i + 1)
                    if s == 1:
                        dve.wait_ge(x_done, i + 1)
                    done["stats", i] = tick(nc.vector.bn_stats(stats[:, i % 2, :], x_sb[:, i, :]))

            def variance(i):
                if 0 <= i < TT:
                    after(("stats", i))
                    done["aggr", i] = tick(nc.vector.bn_aggr(mv[:, i, :], stats[:, i % 2, :]))

            def guarded(i):
                if 0 <= i < TT:
                    after(("aggr", i))
                    done["eps", i] = tick(nc.vector.tensor_scalar_add(var_eps[:, i:i + 1], mv[:, i, 1:2], EPS))

            def inverse(i):
                if 0 <= i < TT:
                    after(("eps", i))
                    nc.vector.reciprocal(rvar[:, i:i + 1], var_eps[:, i:i + 1]).then_inc(rvar_ready, 1)

            for i in range(-1, TT + 2):
                if i == 2 and beside:
                    beside()
                add(i + 1, 0)
                stats_of(i)
                add(i + 1, 1)
                guarded(i - 1)
                add(i + 1, 2)
                variance(i)
                inverse(i - 1)
                if 0 <= i - 2:
                    normalise(dve, s, i - 2)

        def normalise(dve, s, i):
            n = s * TT + i
            dve.wait_ge(rstd_ready, n + 1)
            if s == 1 and i == 0:
                dve.wait_ge(xn_stored[0], 16 * TT)
            if s >= 1:
                dve.wait_ge(xnT_mm, (s - 1) * TT + i + 1)
            nc.vector.tensor_scalar(xn_sb[:, i, :], x_sb[:, i, :], mv[:, i, 0:1], rstd[:, i:i + 1],
                                    ALU.subtract, ALU.mult).then_inc(xn_ready, 1)

        def route_dve(dve, tick, link, l):
            if l == 0:
                dve.wait_ge(const_in, 16 * N_CONST)
            def members(a, b):
                dve.wait_ge(index_ready, l * TT + b)
                link(nc.vector.tensor_copy(ixf[:, a:b, :], top_ix[:, a:b, 0:TOP_K]))
                link(nc.vector.tensor_tensor(chosen[:, a:b], iota_e.unsqueeze(1).unsqueeze(1).broadcast_to([P, b - a, TOP_K, E]),
                                             ixf[:, a:b, :].unsqueeze(3).broadcast_to([P, b - a, TOP_K, E]), ALU.is_equal))
                for h in range(2):
                    ins = nc.vector.tensor_tensor(member2[:, h, a:b, :], chosen[:, a:b, 2 * h, :], chosen[:, a:b, 2 * h + 1, :], ALU.add)
                link(ins)
                return nc.vector.tensor_tensor(member[:, a:b, :], member2[:, 0, a:b, :], member2[:, 1, a:b, :], ALU.add)

            for i in range(TT):
                lg = logit_ps[i][:, 0:E]
                dve.wait_ge(logits_mm, l * TT + i + 1)
                nc.vector.max(top[:, i, :], lg).then_inc(top_ready, 1)
                if i >= 1:
                    top_index(dve, l, i - 1)
                if i == TT - 2:
                    members(0, TT - 2)
            top_index(dve, l, TT - 1)
            members(TT - 2, TT).then_inc(member_ready, 1)
            nc.vector.tensor_tensor(top_rel[:], top[:, :, 0:TOP_K], top[:, :, 0:1].broadcast_to([P, TT, TOP_K]),
                                    ALU.subtract).then_inc(rel_ready, 1)
            dve.wait_ge(rank_mm, l + 1)
            tot = tot_ps[:, 0:TT * E].rearrange("p (e t) -> p e t", t=TT)
            link(nc.vector.tensor_tensor_scan(tot_incl.rearrange("p e t -> p (e t)"), scan_keep_sb[:],
                                              tot_ps[:, 0:TT * E], 0.0, ALU.mult, ALU.add))
            nc.vector.tensor_tensor(tot_excl, tot_incl, tot, ALU.subtract)
            link(nc.vector.tensor_tensor(over, tot_incl[:, :, TT - 1:TT].broadcast_to([P, E, TT]),
                                         thr_sb.unsqueeze(1).broadcast_to([P, E, TT]), ALU.is_gt))
            link(nc.vector.tensor_reduce(ntile[:], over, AX.X, ALU.add))
            link(nc.vector.tensor_tensor_scan(ntile_incl[:], ones_e[:], ntile[:], 0.0, ALU.mult, ALU.add))
            nc.vector.tensor_copy(n_used[:], ntile_incl[0:1, E - 1:E]).then_inc(used_ready, 1)
            link(nc.vector.tensor_tensor(ntile_excl[:], ntile_incl[:], ntile[:], ALU.subtract))
            link(nc.vector.scalar_tensor_tensor(slot_base[:], ntile_excl[:].unsqueeze(2).broadcast_to([P, E, TT]), float(P),
                                                tot_excl, ALU.mult, ALU.add))
            link(nc.vector.tensor_tensor(slot_te[:], rank_ps[:, 0:TT * E].rearrange("p (t e) -> p t e", t=TT),
                                         slot_base[:].rearrange("p e t -> p t e"), ALU.add))
            link(nc.vector.tensor_tensor(slot_pick, chosen, slot_te[:].unsqueeze(2).broadcast_to([P, TT, TOP_K, E]),
                                         ALU.mult))
            link(nc.vector.tensor_reduce(slotf[:], slot_pick.rearrange("p t k e -> p (t k) e"), AX.X, ALU.add))
            link(nc.vector.tensor_copy(slot_ix[:], slotf[:]))
            nc.vector.tensor_single_scalar(slot_qi[:], slot_ix[:], 7, ALU.arith_shift_right)
            link(nc.vector.tensor_single_scalar(slot_ri[:], slot_ix[:], P - 1, ALU.bitwise_and))
            nc.vector.tensor_copy(slot_q[:], slot_qi[:])
            nc.vector.tensor_copy(slot_r[:], slot_ri[:]).then_inc(slot_r_ready, 1)
            dve.wait_ge(slot_r_ready, l + 1)
            slot_q4 = slot_q[:].rearrange("p (t k) -> p t k", k=TOP_K)
            hot_q4 = hot_q.rearrange("p (t k) q -> p t k q", k=TOP_K)
            for k in range(TOP_K):
                equal = tick(nc.vector.tensor_tensor(hot_q4[:, :, k, :], iota16_sb[:, 0:QW].unsqueeze(1).broadcast_to([P, TT, QW]),
                                                     slot_q4[:, :, k].unsqueeze(2).broadcast_to([P, TT, QW]), ALU.is_equal))
                for n in pairs[k * TT:(k + 1) * TT]:
                    if n not in pool_hot:
                        one_hot_r(nc.vector, n).then_inc(hot_r_by_dve, 1)
                dve.wait_ge(dve_step, equal)
                nc.vector.tensor_tensor(hot_q4[:, :, k, :], hot_q4[:, :, k, :], tok1.unsqueeze(2).broadcast_to([P, TT, QW]),
                                        ALU.mult).then_inc(hot_q_ready, 1)
            link(nc.vector.tensor_scalar(tile_ge[:], ntile_incl[0:QW, :], part[0:QW, :], None, ALU.is_le))
            nc.vector.tensor_reduce(tile_e[:], tile_ge[:], AX.X, ALU.add).then_inc(tile_e_ready, 1)
            ids4 = ids_ps[:, 0:TOP_K * QW].rearrange("p (k q) -> p k q", q=QW)
            dve.wait_ge(ids_mm, l + 1)
            link(nc.vector.tensor_reduce(ids_sum[:], ids4.rearrange("p k q -> p q k"), AX.X, ALU.add))
            nc.vector.tensor_scalar(ids[:], ids_sum[:], -1.0, 0.0, ALU.add, ALU.max).then_inc(ids_ready, 1)
            dve.wait_ge(tile_e_mm, l + 1)
            link(nc.vector.tensor_scalar(tile_ec[:, 0, :], tile_ps[0:1, 0:QW], float(E - 1), None, ALU.min))
            nc.vector.tensor_single_scalar(tile_ec[:, 1, :], tile_ec[:, 0, :], 1, ALU.arith_shift_right).then_inc(tiles_ready, 1)
            link(nc.vector.scalar_tensor_tensor(dest_hot, ids4, 0.0, iota_k.unsqueeze(2).broadcast_to([P, TOP_K, QW]),
                                                ALU.is_gt, ALU.mult))
            nc.vector.scalar_tensor_tensor(dest_empty[:], ids_sum[:], 0.0, dump, ALU.is_equal, ALU.mult)
            link(nc.vector.tensor_reduce(dest_k[:], dest_hot.rearrange("p k q -> p q k"), AX.X, ALU.add))
            link(nc.vector.scalar_tensor_tensor(dest_k[:], ids_sum[:], float(TOP_K), dest_k[:], ALU.mult, ALU.add))
            nc.vector.scalar_tensor_tensor(dest[:], dest_k[:], -float(TOP_K), dest_empty[:], ALU.add, ALU.add).then_inc(dest_ready, 1)
            dve.wait_ge(exp_ready, l + 1)
            link(nc.vector.tensor_reduce(top_sum[:], top_exp[:], AX.X, ALU.add))
            link(nc.vector.reciprocal(top_sum[:], top_sum[:]))
            link(nc.vector.scalar_tensor_tensor(wgt[:], top_exp[:], 0.5, top_sum[:].unsqueeze(2).broadcast_to([P, TT, TOP_K]),
                                                ALU.mult, ALU.mult))

        def top_index(dve, l, i):
            dve.wait_ge(top_ready, l * TT + i + 1)
            ins = nc.vector.max_index(top_ix[:, i, :], top[:, i, :], logit_ps[i][:, 0:E])
            ins.then_inc(index_ready, 1)
            return ins

        def experts_dve(dve, l):
            def rows_in(t):
                g, gn = slot_of(l, t, XG)
                s, n = slot_of(l, t)
                dve.wait_ge(xg_used[g], gn + 1)
                dve.wait_ge(h_mm[s], n)
                nc.vector.tensor_copy(xgT[s], xT_ps[s][:, 0:D].rearrange("p (k t) -> p k t", k=KD)).then_inc(xgT_ready[s], 1)

            def hidden_in(t):
                s, n = slot_of(l, t)
                dve.wait_ge(actT_mm[s], n + 1)
                dve.wait_ge(y_mm[s], n)
                nc.vector.tensor_copy(actT[s][0:MI, 0, :], aT_ps[s][0:MI, 0:P])
                nc.vector.tensor_copy(actT[s][:, 1, :], aT_ps[s][:, P:2 * P]).then_inc(actT_ready[s], 1)

            def product(t):
                s, n = slot_of(l, t)
                dve.wait_ge(silu_ready[s], n + 1)
                dve.wait_ge(actT_mm[s], n)
                nc.vector.tensor_tensor(act[s][:, 0:MI], silu_g[s][:, 0:MI], h_ps[s][:, WI:WI + MI], ALU.mult)
                nc.vector.scalar_tensor_tensor(act[s][:, MI:WI], silu_g[s][:, MI:WI], SMALL_SCALE,
                                               h_ps[s][:, WI + MI:2 * WI], ALU.mult, ALU.mult).then_inc(act_ready[s], 1)

            def tiles(a, b):
                for t in range(a, b):
                    rows_in(t)
                    if t >= 2:
                        hidden_in(t - 2)
                    if t >= 1:
                        product(t - 1)

            def drain(t):
                hidden_in(t - 2)
                product(t - 1)
                hidden_in(t - 1)
                skip(dve, l, t, [xgT_ready, actT_ready, act_ready])

            used = tiles_used(dve, l)
            tiles(0, MIN_TILES)
            grouped(dve, used, tiles, drain)

        def combine(dve, l, i, k):
            n = l * TT + i
            if k == 0:
                dve.wait_ge(x_part, n + 1)
            return nc.vector.scalar_tensor_tensor(x_sb[:, i, :], z_sb[n % ZB][:, k, :], wgt[:, i, k:k + 1], x_sb[:, i, :],
                                                  ALU.mult, ALU.add)

        def attention_dve(dve):
            dve.wait_ge(const_in, 16 * (N_CONST + 2))

            def rotate(p):
                if p not in rotated:
                    return
                r = rotated.index(p)
                dve.wait_ge(proj_mm, order.index(p) + 1)
                if r >= 2:
                    dve.wait_ge(roped, r - 1)
                h = DH // 2
                ps = proj_bank[order.index(p)]
                nc.vector.tensor_tensor(rope_a[r % 2], ps[:, :], cos_sb, ALU.mult)
                nc.vector.tensor_tensor(rope_b[r % 2][0:h, :], ps[h:DH, :], sin_sb[h:DH, :], ALU.mult)
                nc.vector.tensor_tensor(rope_b[r % 2][h:DH, :], ps[0:h, :], sin_sb[0:h, :], ALU.mult).then_inc(rope_read, 1)

            def mask(n, c):
                h = n // B
                if c == 0:
                    dve.wait_ge(pv_mm, n)
                    dve.wait_ge(decay_in[h % 2], (h // 2 + 1) * 16)
                dve.wait_ge(scores_mm, 2 * n + c + 1)
                for a, b in ((0, HALF), (HALF, PAIR)):
                    ins = nc.vector.tensor_tensor(probs[c][:, a:b], sc_ps[c][:, a:b], decay_sb[h % 2][:, 0:b - a], ALU.mult)
                if c == 0:
                    ins = nc.vector.tensor_copy(state[n % 2], sc_ps[0][:, PAIR:PAIR + DH])
                ins.then_inc(masked[c], 1)

            def split_output(n):
                dve.wait_ge(o_copied, n + 1)
                if n >= 2:
                    dve.wait_ge(wo_mm, n - 1)
                nc.vector.tensor_tensor(oT_lo[n % 2], o_ps[:, :], oT_hi[n % 2].bitcast(f32), ALU.subtract).then_inc(o_split, 1)

            rotate(("q", 0, 0))
            rotate(("k", 0, 0))
            rotate(("k", 0, 1))
            for n in range(UNITS):
                if n >= 1:
                    split_output(n - 1)
                mask(n, 0)
                for p in projections(n, "scores"):
                    rotate(p)
                mask(n, 1)
                for p in projections(n, "behind"):
                    rotate(p)
            return lambda: split_output(UNITS - 1)

        @block.vector
        def _(dve):
            chain = [0]

            def tick(ins):
                chain[0] += 1
                ins.then_inc(dve_step, 1)
                return chain[0]

            def link(ins):
                dve.wait_ge(dve_step, tick(ins))

            link(nc.vector.memset(ones_e[:], 1.0))
            norm_dve(dve, tick, 0)
            route_dve(dve, tick, link, 0)
            experts_dve(dve, 0)
            norm_dve(dve, tick, 1)
            split_last = attention_dve(dve)
            norm_dve(dve, tick, 2, split_last)
            route_dve(dve, tick, link, 1)
            experts_dve(dve, 1)
            for i in range(0, TT, 2):
                last = {}
                for k in range(TOP_K - 1):
                    for j in (i, i + 1):
                        if k:
                            dve.wait_ge(dve_step, last[j])
                        ins = combine(dve, 1, j, k)
                        if k < TOP_K - 2:
                            last[j] = tick(ins)
                        else:
                            ins.then_inc(x_done, 1)

        def transpose_rows(pe, s, after=None):
            for i in range(TT):
                n = s * TT + i
                pe.wait_ge(xn_ready, n + 1)
                if n >= 2:
                    pe.wait_ge(xnT_copied, n - 1)
                for k in range(KD):
                    ins = nc.tensor.transpose(xT_ps[n % 2][:, k * P:(k + 1) * P], xn_sb[:, i, k * P:(k + 1) * P], ident_sb[:])
                ins.then_inc(xnT_mm, 1)
                if after and i >= 1:
                    after(i - 1)
            if after:
                after(TT - 1)

        def moe_pe(pe, l):
            def logits(i):
                pe.wait_ge(xnT_copied, 2 * l * TT + i + 1)
                if i >= 6:
                    pe.wait_ge(index_ready, l * TT + i - 6 + 1)
                for k in range(KD):
                    ins = nc.tensor.matmul(logit_ps[i][:, 0:E], xnT[:, k, i * P:(i + 1) * P], gate_sb[:, k, :],
                                           start=(k == 0), stop=(k == KD - 1))
                ins.then_inc(logits_mm, 1)
            transpose_rows(pe, 2 * l, logits)
            pe.wait_ge(member_ready, l + 1)
            pe.wait_ge(const_in, 16 * N_CONST)
            mem = member[:].rearrange("p t e -> p (t e)")
            nc.tensor.matmul(rank_ps[:, 0:TT * E], tri_sb[:, 0, :], mem, start=True, stop=True)
            nc.tensor.matmul(tot_ps[:, 0:TT * E], tri_sb[:, 1, :], member[:].rearrange("p t e -> p e t"), start=True, stop=True).then_inc(rank_mm, 1)
            dve_hot = [n for n in pairs if n not in pool_hot]
            for k, i in [(k, i) for k in range(TOP_K) for i in range(TT)]:
                n = i * TOP_K + k
                if i == 0:
                    pe.wait_ge(hot_q_ready, l * TOP_K + k + 1)
                for signal, made in ((hot_r_by_dve, dve_hot), (hot_r_by_pool, pool_hot)):
                    if n in made:
                        pe.wait_ge(signal, l * len(made) + made.index(n) + 1)
                ins = nc.tensor.matmul(ids_ps[:, k * QW:(k + 1) * QW], hot_r[:, n, :], hot_q[:, n, :],
                                       start=(i == 0), stop=(i == TT - 1))
            ins.then_inc(ids_mm, 1)
            pe.wait_ge(tile_e_ready, l + 1)
            nc.tensor.transpose(tile_ps[0:1, 0:QW], tile_e[:, 0:1], ident_sb[0:QW, 0:QW]).then_inc(tile_e_mm, 1)

            pe.wait_ge(tiles_ready, l + 1)
            pe.wait_ge(ids_ready, l + 1)

            def rows_T(t):
                g, gn = slot_of(l, t, XG)
                s, n = slot_of(l, t)
                pe.wait_ge(xg_ready[l][t % XG], (t // XG + 1) * 16)
                pe.wait_ge(xgT_ready[s], n)
                for k in range(KD):
                    ins = nc.tensor.transpose(xT_ps[s][:, k * P:(k + 1) * P], xg[g][:, k * P:(k + 1) * P], ident_sb[:])
                ins.then_inc(xg_used[g], 1)

            def up(t, e, c):
                s, n = slot_of(l, t)
                pe.wait_ge(xgT_ready[s], n + 1)
                pe.wait_ge(act_ready[s], n)
                h2 = h_ps[s][:, 0:2 * WI].rearrange("p (a n) -> p a n", a=2)
                for k in range(KD):
                    w = w_exp_sb[:, bass.ds(e * EXP_COLS + k * 2 * MI, 2 * MI)]
                    nc.tensor.matmul(h2[:, :, 0:MI], xgT[s][:, k, :], w.rearrange("p (a n) -> p a n", a=2), start=(k == 0), stop=(k == KD - 1))
                for k in range(KD):
                    w = w_ch_sb[:, bass.ds(c * CH_COLS + k * 2 * CI, 2 * CI)]
                    ins = nc.tensor.matmul(h2[:, :, MI:WI], xgT[s][:, k, :], w.rearrange("p (a n) -> p a n", a=2), start=(k == 0), stop=(k == KD - 1))
                ins.then_inc(h_mm[s], 1)

            def act_T(t):
                s, n = slot_of(l, t)
                pe.wait_ge(act_ready[s], n + 1)
                pe.wait_ge(actT_ready[s], n)
                nc.tensor.transpose(aT_ps[s][0:MI, 0:P], act[s][:, 0:MI], ident_sb[:])
                nc.tensor.transpose(aT_ps[s][:, P:2 * P], act[s][:, MI:WI], ident_sb[:]).then_inc(actT_mm[s], 1)

            def down(t, e, c):
                s, n = slot_of(l, t)
                pe.wait_ge(actT_ready[s], n + 1)
                if l * SLOT_TILES + t >= 2:
                    pe.wait_ge(y_copied, l * SLOT_TILES + t - 1)
                nc.tensor.matmul(y_ps[s][:, 0:D], actT[s][0:MI, 0, :], w_down_sb[:, bass.ds(e * D, D)], start=True, stop=False)
                nc.tensor.matmul(y_ps[s][:, 0:D], actT[s][:, 1, :],
                                 w_ch_sb[:, bass.ds(c * CH_COLS + KD * 2 * CI, D)],
                                 start=False, stop=True).then_inc(y_mm[s], 1)

            held = {}

            def tiles(a, b):
                for t in range(a, b):
                    rows_T(t)
                    if t >= 2:
                        act_T(t - 2)
                    if t >= 3:
                        down(t - 3, *held[t - 3])
                    if t % LOAD == 0:
                        (_, es), (_, cs) = [nc.values_load_multi_w_load_instructions(
                            tile_ec[0:1, i, t:t + LOAD], engines=(mybir.EngineType.PE,), min_val=0, max_val=most,
                            skip_runtime_bounds_check_because="clamped to E - 1") for i, most in ((0, E - 1), (1, NCH - 1))]
                        for j in range(LOAD):
                            held[t + j] = es[j], cs[j]
                        if l == 1 and t == 0:
                            pe.wait_ge(w_reloaded, 16 * NCH)
                        if l == 0:
                            last = pe.value_load(tile_ec[0:1, 1, t + LOAD - 1:t + LOAD], min_val=0, max_val=NCH - 1)
                            pe.wait_ge(w_ready, last + 1)
                    up(t, *held[t])

            def drain(t):
                act_T(t - 2)
                down(t - 3, *held[t - 3])
                act_T(t - 1)
                down(t - 2, *held[t - 2])
                down(t - 1, *held[t - 1])
                skip(pe, l, t, [xg_used, h_mm, actT_mm, y_mm])

            used = tiles_used(pe, l)
            tiles(0, MIN_TILES)
            grouped(pe, used, tiles, drain)

        def attention_pe(pe):
            def project(p):
                kind, n, b = p
                at = order.index(p)
                if at == 5:
                    pe.wait_ge(kv_copied, 2)
                elif at >= 5 and order[at - 1] in copied:
                    pe.wait_ge(kv_copied, copied.index(order[at - 1]) + 1)
                elif at >= 5:
                    pe.wait_ge(rope_read, rotated.index(order[at - 1]) + 1)
                else:
                    pe.wait_ge(xnT_copied, TT + (b + 1) * SB)
                if kind == "q":
                    key = ("q", n // B)
                elif kind == "k":
                    key = ("k", n)
                if kind == "t":
                    pe.wait_ge(roped, rotated.index(("k", n, b)) + 1)
                    for t in range(2):
                        cols = slice(t * P, (t + 1) * P)
                        ins = nc.tensor.transpose(proj_bank[at][:, cols], kT[n % 2][b][:, cols], ident_sb[:])
                elif kind == "v":
                    pe.wait_ge(kv_in, (n + 1) * 32)
                    for t in range(SB):
                        for k in range(KD):
                            i = b * SB + t
                            ins = nc.tensor.matmul(proj_bank[at][:, t * DH:(t + 1) * DH], xnT[:, k, i * P:(i + 1) * P], wv_sb[:, k, :],
                                                   start=(k == 0), stop=(k == KD - 1))
                else:
                    pe.wait_ge(w_split, split_order.index(key) + 1)
                    pe.wait_ge(xnT_split, (b + 1) * SB)
                    hi, lo = [w.rearrange("p (k n) -> p k n", k=KD)
                              for w in (w_hi[split_buffer(key)], w_lo[split_buffer(key)])]
                    for k in range(KD):
                        for w, x in ((hi, xnT_hi), (lo, xnT_hi), (hi, xnT_lo)):
                            ins = nc.tensor.matmul(proj_bank[at][:, :], w[:, k, :], x[:, k, b * S:(b + 1) * S],
                                                   start=(k == 0 and w is hi and x is xnT_hi), stop=(k == KD - 1 and x is xnT_lo))
                ins.then_inc(proj_mm, 1)

            def scores(n, c):
                g, b = n // GU, n % B
                if c == 0:
                    pe.wait_ge(roped, max(rotated.index(("q", n, b)), rotated.index(("k", g, b))) + 1)
                pe.wait_ge(masked[c], n)
                for t in range(2):
                    j = 2 * c + t
                    ins = nc.tensor.matmul(sc_ps[c][:, t * HALF:t * HALF + HALF - t * P], kT[g % 2][b][:, j * P:(j + 1) * P],
                                           qT[n % 2][:, j * P:(c + 1) * HALF], start=True, stop=True)
                if c == 0:
                    pe.wait_ge(kv_copied, copied.index(("t", g, b)) + 1)
                    pe.wait_ge(v_scaled, n + 1)
                    for t in range(2):
                        ins = nc.tensor.matmul(sc_ps[0][:, PAIR:PAIR + DH], k_tok[g % 2][b][:, t, :], v_dec[n % 2][:, t * DH:(t + 1) * DH],
                                               start=(t == 0), stop=(t == 1))
                ins.then_inc(scores_mm, 1)

            def products(n):
                g, b = n // GU, n % B
                pe.wait_ge(o_split, n)
                if n == 0:
                    pe.wait_ge(rope_read, rotated.index(("k", 0, 1)) + 1)
                if n % GU < B:
                    pe.wait_ge(kv_copied, copied.index(("v", g, b)) + 1)
                for c in range(2):
                    pe.wait_ge(masked[c], n + 1)
                    if c == 1:
                        pe.wait_ge(q_scaled, n + 1)
                        nc.tensor.matmul(o_ps[:, HALF:], state[n % 2], q_dec[n % 2], start=True, stop=False, skip_group_check=True)
                    for t in range(2):
                        j = 2 * c + t
                        ins = nc.tensor.matmul(o_ps[:, j * P:(c + 1) * HALF], v_sb[g % 2][:, b * SB + j, :],
                                               probs[c][:, t * HALF:t * HALF + HALF - t * P],
                                               start=(j == 0), stop=(t == 1), skip_group_check=True)
                ins.then_inc(pv_mm, 1)

            def output(n):
                h = n // B
                key = ("o", h)
                pe.wait_ge(w_split, split_order.index(key) + 1)
                pe.wait_ge(o_split, n + 1)
                hi, lo = w_hi[split_buffer(key)], w_lo[split_buffer(key)]
                for t in range(SB):
                    cols = slice(t * P, (t + 1) * P)
                    for o, w in ((oT_hi, hi), (oT_lo, hi), (oT_hi, lo)):
                        ins = nc.tensor.matmul(res_ps[(n % B) * SB + t], o[n % 2][:, cols], w, start=False, stop=False,
                                               skip_group_check=True)
                ins.then_inc(wo_mm, 1)

            def residual(pair):
                i = 2 * pair
                pe.wait_ge(x_done, i + 2)
                nc.tensor.matmul(bank[4 + pair][:, :], ident_sb[:], x_sb[:, i:i + 2, :], start=True, stop=False, skip_group_check=True)

            def beside(i):
                if i == 2:
                    residual(0)
                if i == 4:
                    residual(1)
                if i == 7:
                    for p in projections(-1, None):
                        project(p)

            transpose_rows(pe, 1, beside)
            for n in range(UNITS):
                scores(n, 0)
                for p in projections(n, "scores"):
                    project(p)
                scores(n, 1)
                if n == 0:
                    residual(3)
                    pe.wait_ge(kv_copied, 1)
                    residual(2)
                if n >= 1:
                    output(n - 1)
                for p in projections(n, "behind"):
                    project(p)
                products(n)
            output(UNITS - 1)

        @block.tensor
        def _(pe):
            pe.wait_ge(gate_in, 32)
            moe_pe(pe, 0)
            attention_pe(pe)
            moe_pe(pe, 1)


def _constants():
    f = np.float32
    half = np.arange(0, DH, 2, dtype=f) / f(DH)
    inv_freq = (f(1.0) / np.power(f(10000.0), half)).astype(f)
    ang = np.arange(S, dtype=f)[:, None] * inv_freq[None, :]
    c, s = np.cos(ang).astype(f).T, np.sin(ang).astype(f).T
    cos = np.concatenate([c, c], 0)
    sin = np.concatenate([s, -s], 0)
    lam = np.exp2(-8.0 * np.arange(1, H + 1, dtype=f) / f(H)).astype(f)
    diff = np.arange(HALF, dtype=f)[None, :] - np.arange(P, dtype=f)[:, None]
    within = np.where(diff[None] >= 0, np.exp(-lam[:, None, None] * np.maximum(diff, 0)[None]), 0.0)
    to_query = np.exp(-lam[:, None, None] * np.arange(1, HALF + 1, dtype=f)[None, None, :]) * np.ones((H, P, 1))
    decay = np.concatenate([within, to_query], 2).astype(f)
    key = (np.arange(P)[:, None, None] + P * np.arange(2)[None, None, :]).astype(f)
    key_decay = np.exp(-lam[None, :, None] * (HALF - 1 - key)).astype(f).reshape(P, 2 * H)
    ident = np.eye(P, dtype=f)
    tri = np.stack([np.triu(np.ones((P, P)), 1), np.ones((P, P))], 1).astype(np.float16)
    p = np.arange(P)[:, None]
    row = lambda a: np.tile(a, (P, 1))
    iotas = np.concatenate([row(np.arange(E)), row(P * np.arange(TT)), p + P * np.arange(TT)[None, :] + 1, row(np.arange(TOP_K)),
                            p, TOP_K * T + p + P * np.arange(QW)[None, :] + TOP_K], 1).astype(f)
    iota16 = row(np.arange(P)).astype(np.float16)
    keep = np.tile(np.tile(np.r_[0.0, np.ones(TT - 1)], E), (P, 1)).astype(f)
    return dict(decay=decay, key_decay=key_decay, cos=cos, sin=sin, ident=ident, tri=tri, iotas=iotas, iota16=iota16, scan_keep=keep)


def kernel(L0_attn_x, L0_attn_wq, L0_attn_wk, L0_attn_wv, L0_attn_wo, L0_ffn_gate_w, L0_ffn_Wg, L0_ffn_Wu, L0_ffn_Wd,
           L0_ffn_cWg, L0_ffn_cWu, L0_ffn_cWd):
    import concourse.bacc as _bacc
    from concourse import mybir as _mybir
    from concourse.bass_utils import run_bass_kernel_spmd as _run

    def contract_first(w, heads):
        w = np.asarray(w)
        return w.reshape(heads, -1, KD, P).transpose(0, 3, 2, 1).reshape(heads, P, -1)

    wg, wu, wd = np.asarray(L0_ffn_Wg), np.asarray(L0_ffn_Wu), np.asarray(L0_ffn_Wd)
    cg, cu, cd = np.asarray(L0_ffn_cWg), np.asarray(L0_ffn_cWu), np.asarray(L0_ffn_cWd)
    up = np.stack([wg, wu], 2).reshape(NCH, 2, KD, P, 2 * MI).transpose(0, 3, 1, 2, 4).reshape(NCH, P, -1)
    cup = np.stack([cg, cu], 2).reshape(NCH, KD, P, 2 * CI).transpose(0, 2, 1, 3).reshape(NCH, P, -1)
    arrays = dict(
        x_in=np.asarray(L0_attn_x).reshape(T, D),
        gate=np.asarray(L0_ffn_gate_w).reshape(E, KD, P).transpose(2, 1, 0),
        w_exp=up, w_ch=np.concatenate([cup, cd], 2),
        w_down=wd.reshape(NCH, 2, MI, D).transpose(0, 2, 1, 3).reshape(NCH, MI, 2 * D),
        wq=contract_first(L0_attn_wq, H), wk=contract_first(L0_attn_wk, HKV), wv=contract_first(L0_attn_wv, HKV),
        wo=np.asarray(L0_attn_wo).reshape(D, H, DH).transpose(1, 2, 0),
        **_constants())
    nc = _bacc.Bacc("TRN2", target_bir_lowering=False, num_devices=1)
    args = {}
    for name, a in arrays.items():
        arrays[name] = a = np.ascontiguousarray(a)
        args[name] = nc.dram_tensor(name, a.shape, _mybir.dt.from_np(a.dtype), kind="ExternalInput").ap()
    args["out"] = nc.dram_tensor("out", (T, D), _mybir.dt.float32, kind="ExternalOutput").ap()
    macaron_kernel(nc, **args)
    r = _run(nc, [arrays], core_ids=[0])
    return r.results[0]["out"].reshape(B, S, D)
```
